# Optimizing a Trainium2 kernel written in Bass

```python
import numpy as np
import jax
import jax.numpy as jnp

def _softmax(x, axis=-1):
    return jax.nn.softmax(x, axis=axis)

def _gelu(x):
    return jax.nn.gelu(x, approximate=True)

def _silu(x):
    return jax.nn.silu(x)

def _sigmoid(x):
    return jax.nn.sigmoid(x)

def _layernorm(x, axis=-1, eps=1e-05):
    m = jnp.mean(x, axis=axis, keepdims=True)
    v = jnp.var(x, axis=axis, keepdims=True)
    return (x - m) / jnp.sqrt(v + eps)

def _scatter_add(tgt, idx, src, axis=0):
    return tgt.at[idx].add(src)

def _segment_sum(src, seg, n):
    return jax.ops.segment_sum(src, seg, n)
kernel_name = 'mk_adaln_d1_jaxref_r4_e501ff'

def setup_inputs(seed: int=0):
    np.random.seed(seed)
    _w = jnp.asarray

    def _L0_attn_setup():
        import jax, jax.numpy as jnp
        import numpy as np
        N_HEAD = 16
        key = jax.random.key(seed)
        k1, k2, k3 = jax.random.split(key, 3)
        B, T, C = (4, 512, 512)
        x = jax.random.normal(k1, (B, T, C), dtype=jnp.float32)
        W_attn = jax.random.normal(k2, (3 * C, C), dtype=jnp.float32) * 0.02
        W_proj = jax.random.normal(k3, (C, C), dtype=jnp.float32) * 0.02
        return {'x': x, 'W_attn': W_attn, 'W_proj': W_proj}
    _L0_attn_in = _L0_attn_setup()

    def _L0_ffn_setup():
        import jax, jax.numpy as jnp
        import numpy as np
        B, P = (32, 64)
        DIMS = [512, 1024, 1024, 512]
        key = jax.random.key(seed)
        ks = jax.random.split(key, 7)

        def lin(k, fan_out, fan_in):
            s = 1.0 / np.sqrt(fan_in)
            return jax.random.uniform(k, (fan_out, fan_in), jnp.float32, -s, s)
        return {'classifier_input': jax.random.normal(ks[0], (B, P, DIMS[0]), jnp.float32), 'W1': lin(ks[1], DIMS[1], DIMS[0]), 'b1': jax.random.uniform(ks[2], (DIMS[1],), jnp.float32, -0.02, 0.02), 'W2': lin(ks[3], DIMS[2], DIMS[1]), 'b2': jax.random.uniform(ks[4], (DIMS[2],), jnp.float32, -0.02, 0.02), 'W3': lin(ks[5], DIMS[3], DIMS[2]), 'b3': jax.random.uniform(ks[6], (DIMS[3],), jnp.float32, -0.02, 0.02)}
    _L0_ffn_in = _L0_ffn_setup()
    _L0_c = _w((lambda *s: np.random.randn(*s).astype(np.float32) * 0.05)(8, 512))
    _L0_wmod = _w((lambda *s: np.random.randn(*s).astype(np.float32) * 0.05)(512, 6 * 512) * 512 ** (-0.5))
    _d = {'L0_attn_x': _L0_attn_in['x'], 'L0_attn_W_attn': _L0_attn_in['W_attn'], 'L0_attn_W_proj': _L0_attn_in['W_proj'], 'L0_ffn_W1': _L0_ffn_in['W1'], 'L0_ffn_b1': _L0_ffn_in['b1'], 'L0_ffn_W2': _L0_ffn_in['W2'], 'L0_ffn_b2': _L0_ffn_in['b2'], 'L0_ffn_W3': _L0_ffn_in['W3'], 'L0_ffn_b3': _L0_ffn_in['b3'], 'L0_c': _L0_c, 'L0_wmod': _L0_wmod}
    _x0 = _d['L0_attn_x']
    _d['L0_attn_x'] = jax.random.normal(jax.random.fold_in(jax.random.key(seed), 1), (8, 512, 512), dtype=_x0.dtype)
    del _x0
    return _d

def reference(L0_attn_x, L0_attn_W_attn, L0_attn_W_proj, L0_ffn_W1, L0_ffn_b1, L0_ffn_W2, L0_ffn_b2, L0_ffn_W3, L0_ffn_b3, L0_c, L0_wmod):

    def _L0_attn_ref(x, W_attn, W_proj):
        import jax, jax.numpy as jnp
        import numpy as np
        N_HEAD = 16
        B, T, C = x.shape
        H = N_HEAD
        d = C // H
        qkv = jnp.einsum('btc,fc->btf', x, W_attn)
        q, k, v = jnp.split(qkv, 3, axis=-1)
        q = q.reshape(B, T, H, d).transpose(0, 2, 1, 3)
        k = k.reshape(B, T, H, d).transpose(0, 2, 1, 3)
        v = v.reshape(B, T, H, d).transpose(0, 2, 1, 3)
        att = jnp.einsum('bhqd,bhkd->bhqk', q, k)
        causal = jnp.tril(jnp.ones((T, T), dtype=bool))
        att = jnp.where(causal, att, -jnp.inf)
        att = jax.nn.softmax(att / jnp.sqrt(jnp.asarray(d, att.dtype)), axis=-1)
        out = jnp.einsum('bhqk,bhkd->bhqd', att, v)
        out = out.transpose(0, 2, 1, 3).reshape(B, T, C)
        return jnp.einsum('btc,oc->bto', out, W_proj)

    def _L0_ffn_ref(classifier_input, W1, b1, W2, b2, W3, b3):
        import jax, jax.numpy as jnp
        import numpy as np
        B, P = (32, 64)
        DIMS = [512, 1024, 1024, 512]
        x = classifier_input
        x = jax.nn.relu(jnp.einsum('bpd,hd->bph', x, W1) + b1)
        x = jax.nn.relu(jnp.einsum('bpd,hd->bph', x, W2) + b2)
        out = jnp.einsum('bpd,od->bpo', x, W3) + b3
        return out
    x = L0_attn_x
    mod = (_silu(L0_c) @ L0_wmod).reshape(L0_c.shape[0], 6, 1, -1)
    sa, ca, ga, sb, cb, gb = (mod[:, 0], mod[:, 1], mod[:, 2], mod[:, 3], mod[:, 4], mod[:, 5])
    ga = (2 * (ga >= 0) - 1) * jnp.maximum(jnp.abs(ga), 0.25)
    gb = (2 * (gb >= 0) - 1) * jnp.maximum(jnp.abs(gb), 0.25)
    h = _layernorm(x, axis=-1) * (1 + ca) + sa
    x = x + ga * _L0_attn_ref(h, L0_attn_W_attn, L0_attn_W_proj)
    h = _layernorm(x, axis=-1) * (1 + cb) + sb
    x = x + gb * _L0_ffn_ref(h, L0_ffn_W1, L0_ffn_b1, L0_ffn_W2, L0_ffn_b2, L0_ffn_W3, L0_ffn_b3)
    return x

_drawn_inputs = setup_inputs


def setup_inputs(seed=0):
    import zlib

    import numpy as np

    out = dict(_drawn_inputs(seed))
    spreads = {}
    factors = {'L0_attn_W_attn': 8.0,
     'L0_attn_W_proj': 8.0,
     'L0_ffn_W1': 10.56,
     'L0_ffn_b1': 64.0,
     'L0_ffn_b2': 64.0,
     'L0_ffn_b3': 63.723,
     'L0_ffn_W2': 2.973}
    for name, (base, spread) in spreads.items():
        noise = np.random.default_rng([zlib.crc32(name.encode()), seed]).standard_normal(out[name].shape)
        drawn = base * np.exp(spread * noise) if base else spread * noise
        out[name] = jnp.asarray(drawn.astype(out[name].dtype))
    for name, factor in factors.items():
        out[name] = (out[name] * factor).astype(out[name].dtype)
    return out
```

```python
from contextlib import ExitStack

import concourse.bass as bass
from concourse import mybir

F32 = mybir.dt.float32
F32R = mybir.dt.float32r
F16 = mybir.dt.float16
BF16 = mybir.dt.bfloat16
ALU = mybir.AluOpType
ACT = mybir.ActivationFunctionType
AX = mybir.AxisListType

P = 128
B, T, C = 8, 512, 512
H, D = 16, 32
F = 1024
NC_ = C // P
NF = F // P
NT = T // P
PAIRS = H // 2
GROUPS = H // 4
UNITS = 5
SOFTMAX_SCALE = float(D) ** -0.5
P_SHIFT = 12 * 0.6931471805599453
MASKED = -1e30
EPS = 1e-5
GATE_FLOOR = 0.25
VW = 3 * D + 1
TERMS = ((0, 0), (0, 1), (1, 0))


def f32(ap):
    return ap.bitcast(F32)


def wait_apart(engine, sem, value, held):
    engine.wait_ge(*held)
    engine.wait_ge(sem, value)


class Memory:

    def __init__(self, nc, ctx):
        self.nc, self.ctx = nc, ctx

    def sb(self, name, shape, dt=F32):
        return self.ctx.enter_context(self.nc.sbuf_tensor(name, shape, dt))

    def banks(self, name, n):
        return [self.ctx.enter_context(self.nc.psum_tensor(f"{name}{i}", [P, 512], F32)) for i in range(n)]

    def sem(self, name):
        return self.ctx.enter_context(self.nc.semaphore(name))


def build(nc, x, wqkv_t, wproj_t, w1_t, b1_c, w2_t, b2_c, w3_t, b3, c_t, wmod, attn_dram, gate_dram, out):
    with ExitStack() as ctx:
        mem = Memory(nc, ctx)
        ident = mem.sb("ident", [P, P])
        mod_cols = mem.sb("mod_cols", [P, 2, 2 * NC_, B])
        with ExitStack() as attention_ctx:
            amem = Memory(nc, attention_ctx)
            wqkv = amem.sb("wqkv", [P, 2, NC_, 3 * C], F32R)
            mask_qk = amem.sb("mask_qk", [P, P], BF16)
            mask_kq = amem.sb("mask_kq", [P, P], BF16)
            ident_bf = amem.sb("ident_bf", [P, P], BF16)
            setup(nc, ident, mod_cols, wqkv, mask_qk, mask_kq, ident_bf, wqkv_t, c_t, wmod, gate_dram)
            attention(nc, amem, x, wqkv, ident, mask_qk, mask_kq, ident_bf, mod_cols, attn_dram)
        with ExitStack() as mlp_ctx:
            mmem = Memory(nc, mlp_ctx)
            wproj = mmem.sb("wproj", [P, 2, NC_, C], F32R)
            w1 = mmem.sb("w1", [P, 2, NC_, F], F32R)
            w2 = mmem.sb("w2", [P, 2, NF, F], F32R)
            w3 = mmem.sb("w3", [P, 2, NF, C], F32R)
            load_mlp_weights(nc, ((wproj_t, wproj), (w1_t, w1), (w2_t, w2), (w3_t, w3)))
            mlp(nc, mmem, x, attn_dram, gate_dram, wproj, w1, w2, w3, b1_c, b2_c, b3, ident, mod_cols, out)


def setup(nc, ident, mod_cols, wqkv, mask_qk, mask_kq, ident_bf, wqkv_t, c_t, wmod, gate_dram):
    SIX = 6 * C
    with ExitStack() as ctx:
        mem = Memory(nc, ctx)
        raw = mem.sb("wqkv_raw", [P, NC_, 3 * C])
        wm = mem.sb("wmod_sb", [P, NC_, SIX])
        cc = mem.sb("c_sb", [P, NC_, B])
        silu = mem.sb("silu", [P, NC_, B])
        rows = mem.sb("mod_rows", [B, SIX])
        flip = mem.sb("gate_abs", [B, 2, C])
        sign = mem.sb("gate_sign", [B, 2, C])
        gates = mem.sb("gates", [B, 2, C])
        psum = mem.banks("mod_psum", 7)
        c_in, gates_out = mem.sem("c_in"), mem.sem("gates_out")
        raw_in = [mem.sem(f"raw_in{c}") for c in range(NC_)]
        wm_in = [mem.sem(f"wm_in{c}") for c in range(NC_)]
        pool_step, exp_done, silu_step, mod_mm, rows_done = (
            mem.sem(n) for n in ("pool_step", "exp_done", "silu_step", "mod_mm", "rows_done"))
        scale_done, gate_step, col_mm, w_hi, w_lo = (
            mem.sem(n) for n in ("scale_done", "gate_step", "col_mm", "w_hi", "w_lo"))

        with nc.Block() as block:
            @block.sync
            def _(sp):
                sp.dma_start(cc[:], c_t.rearrange("(c p) b -> p c b", p=P)).then_inc(c_in, 16)
                for c in range(NC_):
                    sp.dma_start(wm[:, c, :], wmod[c * P:(c + 1) * P, :]).then_inc(wm_in[c], 16)
                for c in range(NC_):
                    sp.dma_start(raw[:, c, :], wqkv_t[c * P:(c + 1) * P, :]).then_inc(raw_in[c], 16)
                sp.wait_ge(gate_step, 5)
                sp.dma_start(gate_dram.rearrange("b (g n) -> b g n", g=2), gates[:]).then_inc(gates_out, 16)
                sp.wait_ge(gates_out, 16)

            @block.gpsimd
            def _(pool):
                nc.gpsimd.memset(ident[:], 0.0).then_inc(pool_step, 1)
                nc.gpsimd.memset(ident_bf[:], 0.0).then_inc(pool_step, 1)
                nc.gpsimd.memset(mask_qk[:], 0.0).then_inc(pool_step, 1)
                nc.gpsimd.memset(mask_kq[:], 0.0).then_inc(pool_step, 1)
                pool.wait_ge(pool_step, 4)
                for m in (ident, ident_bf):
                    nc.gpsimd.affine_select(out=m[:], in_=m[:], compare_op=ALU.not_equal, fill=1.0, base=0,
                                            pattern=[[-1, P]], channel_multiplier=1).then_inc(pool_step, 1)
                nc.gpsimd.affine_select(out=mask_qk[:], in_=mask_qk[:], compare_op=ALU.is_ge, fill=MASKED, base=0,
                                        pattern=[[-1, P]], channel_multiplier=1).then_inc(pool_step, 1)
                nc.gpsimd.affine_select(out=mask_kq[:], in_=mask_kq[:], compare_op=ALU.is_ge, fill=MASKED, base=0,
                                        pattern=[[1, P]], channel_multiplier=-1).then_inc(pool_step, 1)

            @block.scalar
            def _(act):
                act.wait_ge(c_in, 16)
                nc.scalar.activation(silu[:], cc[:], ACT.Exp, scale=-1.0).then_inc(exp_done, 1)
                for c in range(NC_):
                    act.wait_ge(raw_in[c], 16)
                    nc.scalar.copy(wqkv[:, 0, c, :], raw[:, c, :]).then_inc(w_hi, 1)

            @block.vector
            def _(dve):
                dve.wait_ge(exp_done, 1)
                nc.vector.tensor_scalar_add(silu[:], silu[:], 1.0).then_inc(silu_step, 1)
                dve.wait_ge(silu_step, 1)
                nc.vector.reciprocal(silu[:], silu[:]).then_inc(silu_step, 1)
                dve.wait_ge(silu_step, 2)
                nc.vector.tensor_tensor(silu[:], silu[:], cc[:], ALU.mult).then_inc(silu_step, 1)
                for j in range(6):
                    dve.wait_ge(mod_mm, j + 1)
                    nc.vector.tensor_copy(rows[:, j * C:(j + 1) * C], psum[j][0:B, :]).then_inc(rows_done, 1)
                dve.wait_ge(rows_done, 6)
                for j in (1, 4):
                    nc.vector.tensor_scalar_add(rows[:, j * C:(j + 1) * C], rows[:, j * C:(j + 1) * C], 1.0)\
                        .then_inc(scale_done, 1)
                g = rows[:].rearrange("b (s j n) -> b s j n", s=2, j=3)[:, :, 2, :]
                nc.vector.tensor_scalar(sign[:], g, 0.0, 2.0, ALU.is_ge, ALU.mult).then_inc(gate_step, 1)
                nc.vector.scalar_tensor_tensor(out=flip[:], in0=g, scalar=-1.0, in1=g, op0=ALU.mult, op1=ALU.max)\
                    .then_inc(gate_step, 1)
                dve.wait_ge(gate_step, 2)
                nc.vector.tensor_scalar_add(sign[:], sign[:], -1.0).then_inc(gate_step, 1)
                nc.vector.tensor_scalar_max(flip[:], flip[:], GATE_FLOOR).then_inc(gate_step, 1)
                dve.wait_ge(gate_step, 4)
                nc.vector.tensor_tensor(gates[:], sign[:], flip[:], ALU.mult).then_inc(gate_step, 1)
                dve.wait_ge(col_mm, 1)
                nc.vector.tensor_copy(mod_cols[:].rearrange("p s j b -> p (s j b)"), psum[6][:, 0:4 * NC_ * B])
                for c in range(NC_):
                    dve.wait_ge(w_hi, c + 1)
                    nc.vector.tensor_tensor(wqkv[:, 1, c, :], raw[:, c, :], f32(wqkv[:, 0, c, :]), ALU.subtract)\
                        .then_inc(w_lo, 1)

            @block.tensor
            def _(pe):
                pe.wait_ge(silu_step, 3)
                for c in range(NC_):
                    pe.wait_ge(wm_in[c], 16)
                    for j in range(6):
                        mm = nc.tensor.matmul(psum[j][0:B, :], silu[:, c, :], wm[:, c, j * C:(j + 1) * C],
                                              start=(c == 0), stop=(c == NC_ - 1))
                        if c == NC_ - 1:
                            mm.then_inc(mod_mm, 1)
                pe.wait_ge(pool_step, 8)
                pe.wait_ge(scale_done, 2)
                for s in range(2):
                    for j in range(2):
                        for c in range(NC_):
                            at = ((s * 2 + j) * NC_ + c) * B
                            src = (3 * s + j) * C + c * P
                            mm = nc.tensor.transpose(psum[6][:, at:at + B], rows[:, src:src + P], ident[0:B, 0:B])
                mm.then_inc(col_mm, 1)


BY_QUERY = ((0, 0, 3, 0), (1, 0, 2, 0), (1, 0, 0, 384), (2, 1, 3, 0), (3, 1, 2, 0), (3, 1, 0, 384),
            (4, 0, 1, 0), (4, 1, 1, 256))
BY_KEY = tuple((u, h, NT - 1 - t, col) for u, h, t, col in BY_QUERY)
LO_ON_POOL = (1, 3)
LO_ON_DVE = (0, 2, 4)
LAST_SLOT = PAIRS + 2

V_SLOTS = {0: (0, 1), 1: (2,), 2: (3,)}
TURN_SLOT = 3
QK_SLOTS = {4: (0,), 5: (1,), 6: (2,), 7: (3,), 8: (4, 5), 9: (6,), 10: (7,)}
LIN = NC_ + 2 * GROUPS + NT


def attention(nc, mem, x, wqkv, ident, mask_qk, mask_kq, ident_bf, mod_cols, attn_dram):
    xt = mem.sb("x_tiles", [P, NT, C])
    stats = mem.sb("bn_stats", [P, NT, 6])
    mean_var = mem.sb("mean_var", [P, NT, 2])
    var_eps = mem.sb("var_eps", [P, NT])
    rstd = mem.sb("rstd", [P, NT])
    minus_half = mem.sb("minus_half", [P, NT])
    mod_now = mem.sb("mod_now", [P, 2 * NC_])
    full = mem.sb("full", [P, 2, T])
    h = mem.sb("h_parts", [P, 2, NC_, T], F32R)
    qk_parts = mem.sb("qk_parts", [P, 2, 2, T], F32R)
    stack = mem.sb("stack", [P, 2, H, T], F32R)
    v = mem.sb("v_parts", [P, NT, H, VW], BF16)
    row_max = mem.sb("row_max", [P, 2, 2, NT])
    neg_max = mem.sb("neg_max", [P, 2, 2, 2 * NT])
    max_rows = mem.sb("max_rows", [4 * NT, 2, P], F32R)
    prob = mem.sb("prob", [P, UNITS, 512])
    prob_hi = mem.sb("prob_hi", [P, 2, UNITS, 512], F16)
    prob_lo = mem.sb("prob_lo", [P, 2, UNITS, 512], F16)
    o_sum = mem.sb("o_sum", [P, 2, NT, 2, D])
    o_rcp = mem.sb("o_rcp", [P, 2, NT, 2, 1])
    o = mem.sb("o_rows", [P, NT, C])
    score_bank, key_bank, lin_bank = mem.banks("score", 2), mem.banks("key_score", 2), mem.banks("lin", 2)
    o_bank, turn_bank = mem.banks("o_bank", 1)[0], mem.banks("turn", 1)[0]

    x_in = [mem.sem(f"x_in{t}") for t in range(NT)]
    stats_done, aggr_done, var_ready, rstd_ready, x_norm, mod_ready = (
        mem.sem(n) for n in ("stats_done", "aggr_done", "var_ready", "rstd_ready", "x_norm", "mod_ready"))
    lin_done, lin_act, lin_hi, lin_taken = (mem.sem(n) for n in ("lin_done", "lin_act", "lin_hi", "lin_taken"))
    v_rest_ready, v_mid_ready, v_ready = (mem.sem(n) for n in ("v_rest_ready", "v_mid_ready", "v_ready"))
    stack_in = [mem.sem(f"stack_in{g}") for g in range(GROUPS)]
    score_done, score_taken, max_hi, max_ready, turn_done, turn_taken = (
        mem.sem(n) for n in ("score_done", "score_taken", "max_hi", "max_ready", "turn_done", "turn_taken"))
    max_in = [mem.sem(f"max_in{p}") for p in range(PAIRS)]
    key_done, prob_ready, lo_dve, lo_pool, pv_done, o_taken, o_scaled, o_out, consts, consts_dve = (
        mem.sem(n) for n in ("key_done", "prob_ready", "lo_dve", "lo_pool", "pv_done", "o_taken", "o_scaled",
                             "o_out", "consts", "consts_dve"))
    LIN_CREDITS, SCORE_CREDITS, KEY_CREDITS, O_CREDITS, SCALED_CREDITS = 2, 2, 2, 4, 2

    def turn_no(n, c):
        return LIN * n + c

    def qk_no(n, f):
        return LIN * n + NC_ + f

    def v_no(n, t):
        return LIN * n + NC_ + 2 * GROUPS + t

    def unit_no(b, p, u):
        return PAIRS * UNITS * b + UNITS * p + u

    STACK_DMAS = 3 * 4

    def over_batches(engine, body):
        with engine.Fori(0, B - 1) as b:
            body(b, True)
        body(B - 1, False)

    with nc.Block() as block:
        @block.sync
        def _(sp):
            def load_x(n, first):
                if not first:
                    wait_apart(sp, lin_done, turn_no(n - 1, NC_), (o_out, 16))
                for t in range(NT):
                    sp.dma_start(xt[:, t, :], x[n, t * P:(t + 1) * P, :]).then_inc(x_in[t], 16)

            def load_stack(n, g):
                sp.wait_ge(lin_taken, LIN_CREDITS + qk_no(n, 2 * g + 1) + 1)
                for block_row, (q_part, k_part) in enumerate(((0, 0), (1, 0), (0, 1))):
                    for j in range(4):
                        src = f32(qk_parts[32 * j:32 * j + 32, :, :, :]).rearrange("p s l n -> p (s l) n")
                        step = 2 + k_part - q_part
                        sp.dma_start(f32(stack[32 * block_row:32 * block_row + 32, :, 4 * g + j, :]),
                                     src[:, q_part:q_part + step + 1:step, :]).then_inc(stack_in[g], 16)

            sp.sem_inc(o_out, 16)
            load_x(0, True)
            for g in range(GROUPS):
                load_stack(0, g)

            def batch(b, more):
                if more:
                    load_x(b + 1, False)
                for p in range(LAST_SLOT + 1):
                    if more:
                        for f in QK_SLOTS.get(p, ()):
                            if f % 2:
                                load_stack(b + 1, f // 2)
                wait_apart(sp, o_scaled, SCALED_CREDITS + PAIRS * (b + 1), (o_out, 16))
                sp.dma_start(attn_dram[b].rearrange("(t p) n -> p t n", p=P), o[:]).then_inc(o_out, 16)

            over_batches(sp, batch)
            sp.wait_ge(o_out, 16 + 16 * B)

        @block.gpsimd
        def _(pool):
            nc.gpsimd.memset(minus_half[:], -0.5).then_inc(consts, 1)
            pool.wait_ge(consts, 1)
            pool.sem_inc(lo_pool, len(LO_ON_POOL))
            pool.sem_inc(o_scaled, SCALED_CREDITS)

            def inverse_deviation(n):
                pool.wait_ge(var_ready, n + 1)
                nc.gpsimd.tensor_tensor(rstd[:], var_eps[:], minus_half[:], ALU.pow).then_inc(rstd_ready, 1)

            inverse_deviation(0)

            def batch(b, more):
                for p in range(LAST_SLOT + 1):
                    for u in range(UNITS):
                        if 2 <= p < PAIRS + 2 and u in LO_ON_POOL:
                            pool.wait_ge(prob_ready, KEY_CREDITS + unit_no(b, p - 2, u) + 1)
                            nc.gpsimd.tensor_tensor(prob_lo[:, p % 2, u, :], prob[:, u, :], prob_hi[:, p % 2, u, :],
                                                    ALU.subtract).then_inc(lo_pool, 1)
                    if p == 2 and more:
                        inverse_deviation(b + 1)
                    if p >= 3:
                        q = p - 3
                        pool.wait_ge(o_taken, O_CREDITS + H * b + 2 * q + 2)
                        if q == 0:
                            pool.wait_ge(o_out, 16 + 16 * b)
                        nc.gpsimd.tensor_tensor(
                            o[:, :, q * 2 * D:(q + 1) * 2 * D].rearrange("p t (h d) -> p t h d", h=2),
                            o_sum[:, q % 2], o_rcp[:, q % 2].to_broadcast([P, NT, 2, D]), ALU.mult)\
                            .then_inc(o_scaled, 1)

            over_batches(pool, batch)

        @block.scalar
        def _(act):
            act.sem_inc(prob_ready, KEY_CREDITS)
            act.sem_inc(turn_taken, 1)

            def modulate(n, c):
                act.wait_ge(lin_done, turn_no(n, c) + 1)
                if c == 0:
                    act.wait_ge(mod_ready, n + 1)
                nc.scalar.activation(full[:, c % 2, :], lin_bank[c % 2][:], ACT.Identity,
                                     scale=mod_now[:, NC_ + c:NC_ + c + 1], bias=mod_now[:, c:c + 1])\
                    .then_inc(lin_act, 1)

            def qk_hi(n, f, first):
                if f % 2 == 0 and not (first and f == 0):
                    g = f // 2
                    act.wait_ge(stack_in[(g - 1) % GROUPS], 16 * STACK_DMAS * (n + 1 if g else n))
                act.wait_ge(lin_done, qk_no(n, f) + 1)
                nc.scalar.copy(qk_parts[:, f % 2, 0, :], lin_bank[f % 2][:]).then_inc(lin_act, 1)

            def v_high_parts(n, t):
                act.wait_ge(lin_done, v_no(n, t) + 1)
                nc.scalar.copy(v[:, t, :, 0:D], lin_bank[t % 2][:].rearrange("p (h d) -> p h d", h=H))\
                    .then_inc(lin_act, 1)
                act.wait_ge(v_rest_ready, NT * n + t + 1)
                nc.scalar.copy(v[:, t, :, D:2 * D], full[:, t % 2, :].rearrange("p (h d) -> p h d", h=H))\
                    .then_inc(v_mid_ready, 1)

            for c in range(NC_):
                modulate(0, c)
            for f in range(2 * GROUPS):
                qk_hi(0, f, True)

            def batch(b, more):
                for p in range(LAST_SLOT + 1):
                    for u in range(UNITS):
                        if 2 <= p < PAIRS + 2:
                            q = p - 2
                            act.wait_ge(key_done, unit_no(b, q, u) + 1)
                            if u == 0:
                                act.wait_ge(o_taken, O_CREDITS + H * b + 2 * (q - 2) + 2)
                            nc.scalar.activation(prob_hi[:, q % 2, u, :], key_bank[(UNITS * q + u) % 2][:], ACT.Exp,
                                                 scale=SOFTMAX_SCALE, bias=P_SHIFT)
                            if u in LO_ON_DVE:
                                act.wait_ge(lo_dve, len(LO_ON_DVE) * (PAIRS * b + q) + LO_ON_DVE.index(u) + 1)
                            else:
                                act.wait_ge(lo_pool, len(LO_ON_POOL) * (PAIRS * b + q) + LO_ON_POOL.index(u) + 1)
                            nc.scalar.activation(prob[:, u, :], key_bank[(UNITS * q + u) % 2][:], ACT.Exp,
                                                 scale=SOFTMAX_SCALE, bias=P_SHIFT).then_inc(prob_ready, 1)
                        if u == 1 and 1 <= p <= PAIRS:
                            q = p - 1
                            act.wait_ge(turn_done, PAIRS * b + q + 1)
                            nc.scalar.copy(max_rows[:, q % 2, :], turn_bank[0:4 * NT, 0:P]).then_inc(turn_taken, 1)
                            act.wait_ge(turn_taken, 1 + PAIRS * b + q + 1)
                            for part in range(2):
                                act.dma_start(
                                    f32(stack[3 * D + part:3 * D + part + 1, 0, 2 * q:2 * q + 2, :]),
                                    f32(max_rows[2 * NT * part:2 * NT * (part + 1), q % 2, :]))\
                                    .then_inc(max_in[q], 16)
                        if p == TURN_SLOT and more and u < NC_:
                            modulate(b + 1, u)
                    for t in V_SLOTS.get(p, ()):
                        v_high_parts(b, t)
                    if more:
                        for f in QK_SLOTS.get(p, ()):
                            qk_hi(b + 1, f, False)

            over_batches(act, batch)

        @block.vector
        def _(dve):
            nc.vector.memset(f32(stack[3 * D:3 * D + 2, 1, :, :]), 1.0).then_inc(consts_dve, 1)
            nc.vector.memset(v[:, :, :, 3 * D:VW], 1.0).then_inc(consts_dve, 1)
            dve.sem_inc(lin_taken, LIN_CREDITS)
            dve.sem_inc(score_taken, SCORE_CREDITS)
            dve.sem_inc(lo_dve, len(LO_ON_DVE))
            dve.sem_inc(o_taken, O_CREDITS)

            def row_stats(n, t):
                dve.wait_ge(x_in[t], 16 * (n + 1))
                nc.vector.bn_stats(stats[:, t, :], xt[:, t, :]).then_inc(stats_done, 1)
                dve.drain()
                nc.vector.bn_aggr(mean_var[:, t, :], stats[:, t, :]).then_inc(aggr_done, 1)

            def variance(n):
                dve.wait_ge(aggr_done, NT * (n + 1))
                nc.vector.tensor_scalar_add(var_eps[:], mean_var[:, :, 1], EPS).then_inc(var_ready, 1)
                nc.vector.tensor_copy(mod_now[:], mod_cols[:, 0, :, n]).then_inc(mod_ready, 1)

            def normalise(n):
                dve.wait_ge(rstd_ready, n + 1)
                for t in range(NT):
                    nc.vector.tensor_scalar(xt[:, t, :], xt[:, t, :], mean_var[:, t, 0:1], rstd[:, t:t + 1],
                                            ALU.subtract, ALU.mult).then_inc(x_norm, 1)

            def split_h(n, c):
                dve.wait_ge(lin_act, turn_no(n, c) + 1)
                nc.vector.tensor_copy(h[:, 0, c, :], full[:, c % 2, :]).then_inc(lin_hi, 1)
                dve.wait_ge(lin_hi, NC_ * n + c + 1)
                nc.vector.tensor_tensor(h[:, 1, c, :], full[:, c % 2, :], f32(h[:, 0, c, :]), ALU.subtract)\
                    .then_inc(lin_taken, 1)

            def qk_lo(n, f):
                dve.wait_ge(lin_act, qk_no(n, f) + 1)
                nc.vector.tensor_tensor(qk_parts[:, f % 2, 1, :], lin_bank[f % 2][:], f32(qk_parts[:, f % 2, 0, :]),
                                        ALU.subtract).then_inc(lin_taken, 1)

            def v_low_part(n, t):
                def heads(ap):
                    return ap.rearrange("p (h d) -> p h d", h=H)
                dve.wait_ge(lin_act, v_no(n, t) + 1)
                nc.vector.tensor_tensor(heads(full[:, t % 2, :]), heads(lin_bank[t % 2][:]), v[:, t, :, 0:D],
                                        ALU.subtract).then_inc(v_rest_ready, 1)
                dve.wait_ge(v_mid_ready, NT * n + t + 1)
                nc.vector.tensor_tensor(v[:, t, :, 2 * D:3 * D], heads(full[:, t % 2, :]), v[:, t, :, D:2 * D],
                                        ALU.subtract).then_inc(lin_taken, 1)

            for t in range(NT):
                row_stats(0, t)
            variance(0)
            normalise(0)
            for c in range(NC_):
                split_h(0, c)
            for f in range(2 * GROUPS):
                qk_lo(0, f)

            def gather_output(b, head):
                q = head // 2
                dve.wait_ge(pv_done, H * b + head + 1)
                if head % 2 == 0:
                    dve.wait_ge(o_scaled, PAIRS * b + q + 1)
                parts = o_bank[:, 0:NT * VW].rearrange("p (t w) -> p t w", t=NT)
                nc.vector.tensor_reduce(o_sum[:, q % 2, :, head % 2, :],
                                        parts[:, :, 0:3 * D].rearrange("p t (k d) -> p t d k", k=3),
                                        axis=AX.X, op=ALU.add)
                nc.vector.reciprocal(o_rcp[:, q % 2, :, head % 2, :], parts[:, :, 3 * D:VW]).then_inc(o_taken, 1)

            def batch(b, more):
                for p in range(LAST_SLOT + 1):
                    for u in range(UNITS):
                        if p < PAIRS:
                            bank = score_bank[(UNITS * p + u) % 2]
                            dve.wait_ge(score_done, unit_no(b, p, u) + 1)
                            if u == 4:
                                last = nc.vector.reduce_max(row_max[:, p % 2, :, 1], bank[:].rearrange("p (h k) -> p h k", h=2),
                                                            AX.X)
                            else:
                                for _, hh, t, col in (r for r in BY_QUERY if r[0] == u):
                                    last = nc.vector.reduce_max(row_max[:, p % 2, hh, t:t + 1], bank[:, col:col + P * (t + 1)],
                                                                AX.X)
                            last.then_inc(score_taken, 1)
                        if 2 <= p < PAIRS + 2 and u in LO_ON_DVE:
                            dve.wait_ge(prob_ready, KEY_CREDITS + unit_no(b, p - 2, u) + 1)
                            nc.vector.tensor_tensor(prob_lo[:, p % 2, u, :], prob[:, u, :], prob_hi[:, p % 2, u, :],
                                                    ALU.subtract).then_inc(lo_dve, 1)
                        if p >= 3 and u == 1:
                            gather_output(b, 2 * (p - 3))
                        if p >= 3 and u == 3:
                            gather_output(b, 2 * (p - 3) + 1)
                        if p == TURN_SLOT and more and u < NC_:
                            split_h(b + 1, u)
                    if p < PAIRS:
                        dve.wait_ge(score_taken, SCORE_CREDITS + unit_no(b, p, UNITS))
                        peak = row_max[:, p % 2].rearrange("p h t -> p (h t)")
                        nc.vector.tensor_scalar_mul(neg_max[:, p % 2, 0, :].bitcast(F32R), peak, -1.0)\
                            .then_inc(max_hi, 1)
                        dve.wait_ge(max_hi, PAIRS * b + p + 1)
                        nc.vector.scalar_tensor_tensor(
                            out=neg_max[:, p % 2, 1, :].bitcast(F32R), in0=peak, scalar=-1.0,
                            in1=neg_max[:, p % 2, 0, :], op0=ALU.mult, op1=ALU.subtract).then_inc(max_ready, 1)
                    for t in V_SLOTS.get(p, ()):
                        v_low_part(b, t)
                    if more:
                        if p == 0:
                            row_stats(b + 1, 0)
                            row_stats(b + 1, 1)
                        if p == 1:
                            row_stats(b + 1, 2)
                            row_stats(b + 1, 3)
                            variance(b + 1)
                        if p == 2:
                            normalise(b + 1)
                        for f in QK_SLOTS.get(p, ()):
                            qk_lo(b + 1, f)

            over_batches(dve, batch)

        @block.tensor
        def _(pe):
            def turn(n, c):
                if c == 0:
                    pe.wait_ge(x_norm, NT * (n + 1))
                pe.wait_ge(lin_taken, turn_no(n, c) + 1)
                for t in range(NT):
                    mm = nc.tensor.transpose(lin_bank[c % 2][:, t * P:(t + 1) * P], xt[:, t, c * P:(c + 1) * P],
                                             ident[:])
                mm.then_inc(lin_done, 1)

            def qk_terms(n, f, c):
                if c == 0:
                    pe.wait_ge(lin_taken, qk_no(n, f) + 1)
                if f == 0:
                    pe.wait_ge(lin_taken, LIN_CREDITS + turn_no(n, c) + 1)
                at = (f % 2) * C + (f // 2) * P
                for k, (wl, hl) in enumerate(TERMS):
                    mm = nc.tensor.matmul(lin_bank[f % 2][:], wqkv[:, wl, c, at:at + P], h[:, hl, c, :],
                                          start=(c == 0 and k == 0), stop=(c == NC_ - 1 and k == 2))
                if c == NC_ - 1:
                    mm.then_inc(lin_done, 1)

            def v_terms(n, t, c):
                if c == 0:
                    pe.wait_ge(lin_taken, v_no(n, t) + 1)
                for k, (wl, hl) in enumerate(TERMS):
                    mm = nc.tensor.matmul(lin_bank[t % 2][:], h[:, hl, c, t * P:(t + 1) * P], wqkv[:, wl, c, 2 * C:],
                                          start=(c == 0 and k == 0), stop=(c == NC_ - 1 and k == 2))
                if c == NC_ - 1:
                    mm.then_inc(lin_done, 1)

            pe.wait_ge(consts_dve, 2)
            for c in range(NC_):
                turn(0, c)
            for f in range(2 * GROUPS):
                for c in range(NC_):
                    qk_terms(0, f, c)

            def scores_by_query(b, p, u):
                bank = score_bank[(UNITS * p + u) % 2]
                if u == 0:
                    pe.wait_ge(stack_in[p // 2], 16 * STACK_DMAS * (b + 1))
                pe.wait_ge(score_taken, unit_no(b, p, u) + 1)
                for _, hh, t, col in (r for r in BY_QUERY if r[0] == u):
                    head, n = 2 * p + hh, P * (t + 1)
                    nc.tensor.matmul(bank[:, col:col + n], stack[0:3 * D, 0, head, t * P:(t + 1) * P],
                                     stack[0:3 * D, 1, head, 0:n], start=True, stop=False)
                    mm = nc.tensor.matmul(bank[:, col + n - P:col + n], ident_bf[:], mask_qk[:],
                                          start=False, stop=True)
                mm.then_inc(score_done, 1)

            def scores_by_key(b, p, u):
                bank = key_bank[(UNITS * p + u) % 2]
                if u == 0:
                    pe.wait_ge(max_in[p], 32 * (b + 1))
                pe.wait_ge(prob_ready, unit_no(b, p, u) + 1)
                for _, hh, t, col in (r for r in BY_KEY if r[0] == u):
                    head, n = 2 * p + hh, T - P * t
                    nc.tensor.matmul(bank[:, col:col + n], stack[0:3 * D + 2, 1, head, t * P:(t + 1) * P],
                                     stack[0:3 * D + 2, 0, head, t * P:T], start=True, stop=False)
                    mm = nc.tensor.matmul(bank[:, col:col + P], ident_bf[:], mask_kq[:], start=False, stop=True)
                mm.then_inc(key_done, 1)

            def weighted_values(b, p, hh):
                head = 2 * p + hh
                if hh == 0:
                    pe.wait_ge(lo_dve, len(LO_ON_DVE) * (PAIRS * b + p + 2))
                    pe.wait_ge(lo_pool, len(LO_ON_POOL) * (PAIRS * b + p + 2))
                    if p == 0:
                        pe.wait_ge(lin_taken, LIN_CREDITS + v_no(b, NT))
                pe.wait_ge(o_taken, O_CREDITS + H * b + head)
                place = {t: (u, col) for u, h2, t, col in BY_KEY if h2 == hh}
                for i in range(NT):
                    for j in range(i + 1):
                        u, col = place[j]
                        at = col + P * (i - j)
                        for part in (prob_hi, prob_lo):
                            mm = nc.tensor.matmul(o_bank[:, i * VW:(i + 1) * VW], part[:, p % 2, u, at:at + P],
                                                  v[:, j, head, :], start=(j == 0 and part is prob_hi),
                                                  stop=(j == i and part is prob_lo))
                mm.then_inc(pv_done, 1)

            def batch(b, more):
                for p in range(LAST_SLOT + 1):
                    for u in range(UNITS):
                        if p < PAIRS:
                            scores_by_query(b, p, u)
                        if 2 <= p < PAIRS + 2:
                            scores_by_key(b, p - 2, u)
                        if p >= 3 and u == 0:
                            weighted_values(b, p - 3, 0)
                        if u == 1 and 1 <= p <= PAIRS:
                            q = p - 1
                            pe.wait_ge(max_ready, PAIRS * b + q + 1)
                            pe.wait_ge(turn_taken, PAIRS * b + q + 1)
                            nc.tensor.transpose(turn_bank[0:4 * NT, 0:P],
                                                neg_max[:, q % 2, :, :].rearrange("p l m -> p (l m)"), ident[:])\
                                .then_inc(turn_done, 1)
                        if p >= 3 and u == 2:
                            weighted_values(b, p - 3, 1)
                        if u < NC_:
                            for t in V_SLOTS.get(p, ()):
                                v_terms(b, t, u)
                            if p == TURN_SLOT and more:
                                turn(b + 1, u)
                            if more:
                                for f in QK_SLOTS.get(p, ()):
                                    qk_terms(b + 1, f, u)

            over_batches(pe, batch)


def load_mlp_weights(nc, weights):
    SLOTS = 6
    with ExitStack() as ctx:
        mem = Memory(nc, ctx)
        raw = mem.sb("w_raw", [P, SLOTS, F])
        raw_in = [mem.sem(f"w_raw_in{i}") for i in range(SLOTS)]
        hi_done, lo_done = mem.sem("w_hi_done"), mem.sem("w_lo_done")
        strips = [(src, dst, c) for src, dst in weights for c in range(src.shape[0] // P)]

        with nc.Block() as block:
            @block.sync
            def _(sp):
                for i, (src, dst, c) in enumerate(strips):
                    if i >= SLOTS:
                        sp.wait_ge(lo_done, i - SLOTS + 1)
                    sp.dma_start(raw[:, i % SLOTS, 0:src.shape[1]], src[c * P:(c + 1) * P, :])\
                        .then_inc(raw_in[i % SLOTS], 16)

            @block.scalar
            def _(act):
                for i, (src, dst, c) in enumerate(strips):
                    act.wait_ge(raw_in[i % SLOTS], 16 * (i // SLOTS + 1))
                    nc.scalar.copy(dst[:, 0, c, :], raw[:, i % SLOTS, 0:src.shape[1]]).then_inc(hi_done, 1)

            @block.vector
            def _(dve):
                for i, (src, dst, c) in enumerate(strips):
                    dve.wait_ge(hi_done, i + 1)
                    nc.vector.tensor_tensor(dst[:, 1, c, :], raw[:, i % SLOTS, 0:src.shape[1]], f32(dst[:, 0, c, :]),
                                            ALU.subtract).then_inc(lo_done, 1)


CH = 256
CT = CH // P
HALVES = T // CH
FB = NC_ + 2 * NF
TB = NC_ + 2 * CT
PROJ_AFTER = 2
NORM_AFTER = 4


def mlp(nc, mem, x, attn_dram, gate_dram, wproj, w1, w2, w3, b1_c, b2_c, b3, ident, mod_cols, out):
    ga = mem.sb("gate_attn", [P, C])
    gb = mem.sb("gate_mlp", [P, C])
    b3_rows = mem.sb("b3_rows", [P, C])
    b1_cols = mem.sb("b1_cols", [P, NF])
    b2_cols = mem.sb("b2_cols", [P, NF])
    mod_now = mem.sb("mlp_mod_now", [P, 2 * NC_])
    at = mem.sb("attn_tiles", [P, CT, C])
    xt = mem.sb("res_tiles", [P, HALVES, CT, C])
    a = mem.sb("turned", [P, 2, NC_, CH], F32R)
    y1 = mem.sb("y1", [P, 2, NF, CH], F32R)
    y2 = mem.sb("y2", [P, 2, NF, CH], F32R)
    full = mem.sb("mlp_full", [P, 2, CH])
    gated = mem.sb("gated", [P, C])
    stats = mem.sb("mlp_stats", [P, CT, 6])
    mean_var = mem.sb("mlp_mean_var", [P, CT, 2])
    var_eps = mem.sb("mlp_var_eps", [P, CT])
    rstd = mem.sb("mlp_rstd", [P, CT])
    minus_half = mem.sb("mlp_minus_half", [P, CT])
    fbank, tbank = mem.banks("feature", 4), mem.banks("token", 4)

    const_in, ga_in, gb_in = mem.sem("const_in"), mem.sem("ga_in"), mem.sem("gb_in")
    at_in = mem.sem("at_in")
    res_in = [mem.sem(f"res_in{h}") for h in range(HALVES)]
    out_done = [mem.sem(f"out_done{h}") for h in range(HALVES)]
    (f_done, f_act, f_hi, f_split, t_done, t_act, t_taken, gate_step, x2_ready, stats_done, aggr_done, var_ready,
     rstd_ready, x_norm, mod_ready, out_step, out_ready, consts) = (mem.sem(n) for n in (
         "f_done", "f_act", "f_hi", "f_split", "t_done", "t_act", "t_taken", "gate_step", "x2_ready",
         "mlp_stats_done", "mlp_aggr_done", "mlp_var_ready", "mlp_rstd_ready", "mlp_x_norm", "mlp_mod_ready",
         "out_step", "out_ready", "mlp_consts"))
    F_CREDITS, FULL_CREDITS, T_CREDITS = 4, 2, 4

    def rows_no(k, c):
        return FB * k + c

    def layer_no(k, layer, f):
        return FB * k + NC_ + NF * (layer - 1) + f

    def turned_no(k, c):
        return TB * k + c if k_is_first(k) else TB * k - CT + c

    def k_is_first(k):
        return isinstance(k, int) and k == 0

    def proj_no(k, t):
        return turned_no(k, NC_) + t

    def last_no(k, t, more):
        return TB * k + NC_ + CT + (NC_ + CT if more else 0) + t

    def over_chunks(engine, body):
        with engine.Fori(0, B - 1) as b:
            for half in range(HALVES):
                body(HALVES * b + half, b, half, True)
        for half in range(HALVES):
            body(HALVES * (B - 1) + half, B - 1, half, half < HALVES - 1)

    def following(b, half):
        return (b, half + 1) if half < HALVES - 1 else (b + 1, 0)

    def fbank_of(k_even_no):
        return fbank[k_even_no % 4]

    def tiles(dram, b, half):
        return dram[b, half * CH:(half + 1) * CH, :].rearrange("(t p) n -> p t n", p=P)

    with nc.Block() as block:
        @block.sync
        def _(sp):
            def load_gate(tile, b, which, sem):
                sp.dma_start(tile[:], gate_dram[b:b + 1, which * C:(which + 1) * C].to_broadcast([P, C])
                             if isinstance(b, int) else
                             gate_dram[bass.ds(b, 1), which * C:(which + 1) * C].to_broadcast([P, C])).then_inc(sem, 16)

            def load_attn(b, half):
                sp.dma_start(at[:], tiles(attn_dram, b, half)).then_inc(at_in, 16)

            def load_x(b, half):
                sp.dma_start(xt[:, half], tiles(x, b, half)).then_inc(res_in[half], 16)

            held = (out_done[0], 16)
            load_attn(0, 0)
            load_x(0, 0)
            load_gate(ga, 0, 0, ga_in)
            load_gate(gb, 0, 1, gb_in)
            sp.dma_start(b1_cols[:], b1_c).then_inc(const_in, 16)
            sp.dma_start(b2_cols[:], b2_c).then_inc(const_in, 16)
            sp.dma_start(b3_rows[:], b3.to_broadcast([P, C])).then_inc(const_in, 16)

            def chunk(k, b, half, more):
                nb, nh = following(b, half)
                if more:
                    wait_apart(sp, f_done, rows_no(k, NC_), held)
                    load_attn(nb, nh)
                    wait_apart(sp, out_done[nh], 16 * (b + half + 1), held)
                    load_x(nb, nh)
                    if nh == 0:
                        wait_apart(sp, t_taken, T_CREDITS + proj_no(k, CT), held)
                        load_gate(ga, nb, 0, ga_in)
                if more and nh == 0:
                    sp.wait_ge(out_ready, CT * (k + 1))
                    load_gate(gb, nb, 1, gb_in)

            over_chunks(sp, chunk)

        @block.gpsimd
        def _(pool):
            nc.gpsimd.memset(minus_half[:], -0.5).then_inc(consts, 1)
            pool.wait_ge(consts, 1)

            def inverse_deviation(k):
                pool.wait_ge(var_ready, k + 1)
                nc.gpsimd.tensor_tensor(rstd[:], var_eps[:], minus_half[:], ALU.pow).then_inc(rstd_ready, 1)

            inverse_deviation(0)

            def chunk(k, b, half, more):
                if more:
                    inverse_deviation(k + 1)

            over_chunks(pool, chunk)

        @block.scalar
        def _(act):
            act.sem_inc(f_act, F_CREDITS)
            for half in range(HALVES):
                act.sem_inc(out_done[half], 16)

            def turned_hi(k, c, at_no):
                act.wait_ge(t_done, turned_no(k, c) + 1)
                nc.scalar.copy(a[:, 0, c, :], tbank[at_no % 4][:, 0:CH]).then_inc(t_act, 1)

            def modulate(k, b, c):
                act.wait_ge(f_done, rows_no(k, c) + 1)
                act.wait_ge(f_split, rows_no(k, c) + 1)
                if c == 0:
                    act.wait_ge(mod_ready, b + 1)
                nc.scalar.activation(full[:, c % 2, :], fbank[c % 4][:, 0:CH], ACT.Identity,
                                     scale=mod_now[:, NC_ + c:NC_ + c + 1], bias=mod_now[:, c:c + 1])\
                    .then_inc(f_act, 1)

            def hidden(k, layer, f):
                act.wait_ge(f_done, layer_no(k, layer, f) + 1)
                act.wait_ge(f_split, layer_no(k, layer, f) + 1)
                bias = (b1_cols, b2_cols)[layer - 1]
                nc.scalar.activation(full[:, f % 2, :], fbank[f % 4][:, 0:CH], ACT.Relu, bias=bias[:, f:f + 1])\
                    .then_inc(f_act, 1)

            act.wait_ge(const_in, 48)
            for c in range(NC_):
                turned_hi(0, c, c)
            for c in range(NC_):
                modulate(0, 0, c)

            def chunk(k, b, half, more):
                nb, nh = following(b, half)
                for f in range(NF):
                    hidden(k, 1, f)
                if more:
                    for c in range(NC_):
                        turned_hi(k + 1, c, turned_no(1, c))
                for f in range(NF):
                    hidden(k, 2, f)
                if more:
                    for c in range(NC_):
                        modulate(k + 1, nb, c)
                act.wait_ge(out_ready, CT * (k + 1))
                act.dma_start(tiles(out, b, half), xt[:, half]).then_inc(out_done[half], 16)

            over_chunks(act, chunk)
            for half in range(HALVES):
                act.wait_ge(out_done[half], 16 * (B + 1))

        @block.vector
        def _(dve):
            dve.sem_inc(f_split, FULL_CREDITS)
            dve.sem_inc(t_taken, T_CREDITS)

            def turned_lo(k, c, at_no):
                dve.wait_ge(t_act, NC_ * k + c + 1)
                nc.vector.tensor_tensor(a[:, 1, c, :], tbank[at_no % 4][:, 0:CH], f32(a[:, 0, c, :]), ALU.subtract)\
                    .then_inc(t_taken, 1)

            def split(dst, c, number, ring):
                dve.wait_ge(f_act, F_CREDITS + number + 1)
                nc.vector.tensor_copy(dst[:, 0, c, :], full[:, ring, :]).then_inc(f_hi, 1)
                dve.wait_ge(f_hi, number + 1)
                nc.vector.tensor_tensor(dst[:, 1, c, :], full[:, ring, :], f32(dst[:, 0, c, :]), ALU.subtract)\
                    .then_inc(f_split, 1)

            def add_attention(k, b, half, t, at_no):
                dve.wait_ge(t_done, proj_no(k, t) + 1)
                if half == 0 and t == 0:
                    dve.wait_ge(ga_in, 16 * (b + 1))
                nc.vector.tensor_tensor(gated[:], tbank[at_no % 4][:], ga[:], ALU.mult).then_inc(t_taken, 1)
                dve.wait_ge(t_taken, T_CREDITS + proj_no(k, t) + 1)
                dve.wait_ge(res_in[half], 16 * (b + 1))
                nc.vector.tensor_tensor(xt[:, half, t, :], xt[:, half, t, :], gated[:], ALU.add).then_inc(x2_ready, 1)
                dve.wait_ge(x2_ready, CT * k + t + 1)
                nc.vector.bn_stats(stats[:, t, :], xt[:, half, t, :]).then_inc(stats_done, 1)
                dve.drain()
                nc.vector.bn_aggr(mean_var[:, t, :], stats[:, t, :]).then_inc(aggr_done, 1)

            def variance(k):
                dve.wait_ge(aggr_done, CT * (k + 1))
                nc.vector.tensor_scalar_add(var_eps[:], mean_var[:, :, 1], EPS).then_inc(var_ready, 1)

            def normalise(k, b, half):
                dve.wait_ge(rstd_ready, k + 1)
                for t in range(CT):
                    nc.vector.tensor_scalar(at[:, t, :], xt[:, half, t, :], mean_var[:, t, 0:1], rstd[:, t:t + 1],
                                            ALU.subtract, ALU.mult).then_inc(x_norm, 1)
                if half == 0:
                    nc.vector.tensor_copy(mod_now[:], mod_cols[:, 1, :, b]).then_inc(mod_ready, 1)

            def finish(k, b, half, t, more):
                dve.wait_ge(t_done, last_no(k, t, more) + 1)
                if half == 0 and t == 0:
                    dve.wait_ge(gb_in, 16 * (b + 1))
                if t:
                    dve.wait_ge(out_ready, CT * k + t)
                nc.vector.tensor_tensor(gated[:], tbank[last_no(0, t, more) % 4][:], b3_rows[:], ALU.add).then_inc(t_taken, 1)
                dve.wait_ge(t_taken, T_CREDITS + last_no(k, t, more) + 1)
                nc.vector.tensor_tensor(gated[:], gated[:], gb[:], ALU.mult).then_inc(out_step, 1)
                dve.wait_ge(out_step, CT * k + t + 1)
                nc.vector.tensor_tensor(xt[:, half, t, :], xt[:, half, t, :], gated[:], ALU.add).then_inc(out_ready, 1)

            dve.wait_ge(const_in, 48)
            for c in range(NC_):
                turned_lo(0, c, c)
            for t in range(CT):
                add_attention(0, 0, 0, t, NC_ + t)
            variance(0)
            normalise(0, 0, 0)
            for c in range(NC_):
                split(a, c, rows_no(0, c), c % 2)

            def chunk(k, b, half, more):
                nb, nh = following(b, half)
                for f in range(NF):
                    split(y1, f, layer_no(k, 1, f), f % 2)
                if more:
                    for c in range(NC_):
                        turned_lo(k + 1, c, turned_no(1, c))
                for f in range(NF):
                    split(y2, f, layer_no(k, 2, f), f % 2)
                    if more and f == PROJ_AFTER - 1:
                        for t in range(CT):
                            add_attention(k + 1, nb, nh, t, proj_no(1, t))
                        variance(k + 1)
                    if more and f == NORM_AFTER - 1:
                        normalise(k + 1, nb, nh)
                if more:
                    for c in range(NC_):
                        split(a, c, rows_no(k + 1, c), c % 2)
                for t in range(CT):
                    finish(k, b, half, t, more)

            over_chunks(dve, chunk)

        @block.tensor
        def _(pe):
            def turn_attention(k, c, at_no):
                if c == 0:
                    pe.wait_ge(at_in, 16 * (k + 1))
                pe.wait_ge(t_taken, turned_no(k, c) + 1)
                for t in range(CT):
                    mm = nc.tensor.transpose(tbank[at_no % 4][:, t * P:(t + 1) * P], at[:, t, c * P:(c + 1) * P],
                                             ident[:])
                mm.then_inc(t_done, 1)

            def turn_rows(k, c):
                if c == 0:
                    pe.wait_ge(x_norm, CT * (k + 1))
                pe.wait_ge(f_act, rows_no(k, c) + 1)
                for t in range(CT):
                    mm = nc.tensor.transpose(fbank[c % 4][:, t * P:(t + 1) * P], at[:, t, c * P:(c + 1) * P], ident[:])
                mm.then_inc(f_done, 1)

            def token_rows(weights, data, chunks, t, bank, number, ready):
                pe.wait_ge(t_taken, number + 1)
                for c in range(chunks):
                    if t == 0:
                        ready(c)
                    for i, (wl, dl) in enumerate(TERMS):
                        mm = nc.tensor.matmul(bank[:], data[:, dl, c, t * P:(t + 1) * P], weights[:, wl, c, :],
                                              start=(c == 0 and i == 0), stop=(c == chunks - 1 and i == 2))
                mm.then_inc(t_done, 1)

            def project(k, t, at_no):
                token_rows(wproj, a, NC_, t, tbank[at_no % 4], proj_no(k, t),
                           lambda c: pe.wait_ge(t_taken, T_CREDITS + turned_no(k, c) + 1))

            def last_layer(k, t, more):
                token_rows(w3, y2, NF, t, tbank[last_no(0, t, more) % 4], last_no(k, t, more),
                           lambda c: pe.wait_ge(f_split, FULL_CREDITS + layer_no(k, 2, c) + 1))

            def hidden(k, layer, f):
                weights, data, chunks = ((w1, a, NC_), (w2, y1, NF))[layer - 1]
                pe.wait_ge(f_act, layer_no(k, layer, f) + 1)
                for c in range(chunks):
                    if f == 0:
                        pe.wait_ge(f_split, FULL_CREDITS + 1 + (rows_no(k, c) if layer == 1 else layer_no(k, 1, c)))
                    for i, (wl, dl) in enumerate(TERMS):
                        mm = nc.tensor.matmul(fbank[f % 4][:, 0:CH], weights[:, wl, c, f * P:(f + 1) * P],
                                              data[:, dl, c, :], start=(c == 0 and i == 0),
                                              stop=(c == chunks - 1 and i == 2))
                mm.then_inc(f_done, 1)

            for c in range(NC_):
                turn_attention(0, c, c)
            for t in range(CT):
                project(0, t, NC_ + t)
            for c in range(NC_):
                turn_rows(0, c)

            def chunk(k, b, half, more):
                for f in range(NF):
                    hidden(k, 1, f)
                if more:
                    for c in range(NC_):
                        turn_attention(k + 1, c, turned_no(1, c))
                for f in range(NF):
                    hidden(k, 2, f)
                    if more and f == PROJ_AFTER - 1:
                        for t in range(CT):
                            project(k + 1, t, proj_no(1, t))
                if more:
                    for c in range(NC_):
                        turn_rows(k + 1, c)
                for t in range(CT):
                    last_layer(k, t, more)

            over_chunks(pe, chunk)


def kernel(L0_attn_x, L0_attn_W_attn, L0_attn_W_proj, L0_ffn_W1, L0_ffn_b1, L0_ffn_W2, L0_ffn_b2, L0_ffn_W3,
           L0_ffn_b3, L0_c, L0_wmod):
    import numpy as np
    import concourse.bacc as bacc
    from concourse.bass_utils import run_bass_kernel_spmd

    arrays = {
        "x": L0_attn_x, "wqkv_t": np.asarray(L0_attn_W_attn).T, "wproj_t": np.asarray(L0_attn_W_proj).T,
        "w1_t": np.asarray(L0_ffn_W1).T, "b1_c": np.asarray(L0_ffn_b1).reshape(NF, P).T,
        "w2_t": np.asarray(L0_ffn_W2).T, "b2_c": np.asarray(L0_ffn_b2).reshape(NF, P).T,
        "w3_t": np.asarray(L0_ffn_W3).T, "b3": np.asarray(L0_ffn_b3).reshape(1, C),
        "c_t": np.asarray(L0_c).T, "wmod": L0_wmod,
    }
    arrays = {k: np.ascontiguousarray(a) for k, a in arrays.items()}
    nc = bacc.Bacc("TRN2", target_bir_lowering=False, num_devices=1)
    ins = {k: nc.dram_tensor(k, a.shape, mybir.dt.from_np(a.dtype), kind="ExternalInput").ap()
           for k, a in arrays.items()}
    attn_dram = nc.dram_tensor("attn_dram", (B, T, C), F32, kind="Internal").ap()
    gate_dram = nc.dram_tensor("gate_dram", (B, 2 * C), F32, kind="Internal").ap()
    out = nc.dram_tensor("out", (B, T, C), F32, kind="ExternalOutput").ap()
    build(nc, attn_dram=attn_dram, gate_dram=gate_dram, out=out, **ins)
    result = run_bass_kernel_spmd(nc, [arrays], core_ids=[0])
    return result.results[0]["out"]
```

```python
from contextlib import ExitStack

import concourse.bass as bass
from concourse import mybir

F32 = mybir.dt.float32
F32R = mybir.dt.float32r
F16 = mybir.dt.float16
BF16 = mybir.dt.bfloat16
ALU = mybir.AluOpType
ACT = mybir.ActivationFunctionType
AX = mybir.AxisListType

P = 128
B, T, C = 8, 512, 512
H, D = 16, 32
F = 1024
NC_ = C // P
NF = F // P
NT = T // P
PAIRS = H // 2
GROUPS = H // 4
UNITS = 5
SOFTMAX_SCALE = float(D) ** -0.5
P_SHIFT = 12 * 0.6931471805599453
MASKED = -1e30
EPS = 1e-5
GATE_FLOOR = 0.25
VW = 3 * D + 1
TERMS = ((0, 0), (0, 1), (1, 0))


def f32(ap):
    return ap.bitcast(F32)


def wait_apart(engine, sem, value, held):
    engine.wait_ge(*held)
    engine.wait_ge(sem, value)


class Memory:

    def __init__(self, nc, ctx):
        self.nc, self.ctx = nc, ctx

    def sb(self, name, shape, dt=F32):
        return self.ctx.enter_context(self.nc.sbuf_tensor(name, shape, dt))

    def banks(self, name, n):
        return [self.ctx.enter_context(self.nc.psum_tensor(f"{name}{i}", [P, 512], F32)) for i in range(n)]

    def sem(self, name):
        return self.ctx.enter_context(self.nc.semaphore(name))


def build(nc, x, wqkv_t, wproj_t, w1_t, b1_c, w2_t, b2_c, w3_t, b3, c_t, wmod, attn_dram, gate_dram, out):
    with ExitStack() as ctx:
        mem = Memory(nc, ctx)
        ident = mem.sb("ident", [P, P])
        mod_cols = mem.sb("mod_cols", [P, 2, 2 * NC_, B])
        with ExitStack() as attention_ctx:
            amem = Memory(nc, attention_ctx)
            wqkv = amem.sb("wqkv", [P, 2, NC_, 3 * C], F32R)
            mask_qk = amem.sb("mask_qk", [P, P], BF16)
            mask_kq = amem.sb("mask_kq", [P, P], BF16)
            ident_bf = amem.sb("ident_bf", [P, P], BF16)
            setup(nc, ident, mod_cols, wqkv, mask_qk, mask_kq, ident_bf, wqkv_t, c_t, wmod, gate_dram)
            attention(nc, amem, x, wqkv, ident, mask_qk, mask_kq, ident_bf, mod_cols, attn_dram)
        with ExitStack() as mlp_ctx:
            mmem = Memory(nc, mlp_ctx)
            wproj = mmem.sb("wproj", [P, 2, NC_, C], F32R)
            w1 = mmem.sb("w1", [P, 2, NC_, F], F32R)
            w2 = mmem.sb("w2", [P, 2, NF, F], F32R)
            w3 = mmem.sb("w3", [P, 2, NF, C], F32R)
            load_mlp_weights(nc, ((wproj_t, wproj), (w1_t, w1), (w2_t, w2), (w3_t, w3)))
            mlp(nc, mmem, x, attn_dram, gate_dram, wproj, w1, w2, w3, b1_c, b2_c, b3, ident, mod_cols, out)


def setup(nc, ident, mod_cols, wqkv, mask_qk, mask_kq, ident_bf, wqkv_t, c_t, wmod, gate_dram):
    SIX = 6 * C
    with ExitStack() as ctx:
        mem = Memory(nc, ctx)
        raw = mem.sb("wqkv_raw", [P, NC_, 3 * C])
        wm = mem.sb("wmod_sb", [P, NC_, SIX])
        cc = mem.sb("c_sb", [P, NC_, B])
        silu = mem.sb("silu", [P, NC_, B])
        rows = mem.sb("mod_rows", [B, SIX])
        flip = mem.sb("gate_abs", [B, 2, C])
        sign = mem.sb("gate_sign", [B, 2, C])
        gates = mem.sb("gates", [B, 2, C])
        psum = mem.banks("mod_psum", 7)
        c_in, gates_out = mem.sem("c_in"), mem.sem("gates_out")
        raw_in = [mem.sem(f"raw_in{c}") for c in range(NC_)]
        wm_in = [mem.sem(f"wm_in{c}") for c in range(NC_)]
        pool_step, exp_done, silu_step, mod_mm, rows_done = (
            mem.sem(n) for n in ("pool_step", "exp_done", "silu_step", "mod_mm", "rows_done"))
        scale_done, gate_step, col_mm, w_hi, w_lo = (
            mem.sem(n) for n in ("scale_done", "gate_step", "col_mm", "w_hi", "w_lo"))

        with nc.Block() as block:
            @block.sync
            def _(sp):
                sp.dma_start(cc[:], c_t.rearrange("(c p) b -> p c b", p=P)).then_inc(c_in, 16)
                for c in range(NC_):
                    sp.dma_start(wm[:, c, :], wmod[c * P:(c + 1) * P, :]).then_inc(wm_in[c], 16)
                for c in range(NC_):
                    sp.dma_start(raw[:, c, :], wqkv_t[c * P:(c + 1) * P, :]).then_inc(raw_in[c], 16)
                sp.wait_ge(gate_step, 5)
                sp.dma_start(gate_dram.rearrange("b (g n) -> b g n", g=2), gates[:]).then_inc(gates_out, 16)
                sp.wait_ge(gates_out, 16)

            @block.gpsimd
            def _(pool):
                nc.gpsimd.memset(ident[:], 0.0).then_inc(pool_step, 1)
                nc.gpsimd.memset(ident_bf[:], 0.0).then_inc(pool_step, 1)
                nc.gpsimd.memset(mask_qk[:], 0.0).then_inc(pool_step, 1)
                nc.gpsimd.memset(mask_kq[:], 0.0).then_inc(pool_step, 1)
                pool.wait_ge(pool_step, 4)
                for m in (ident, ident_bf):
                    nc.gpsimd.affine_select(out=m[:], in_=m[:], compare_op=ALU.not_equal, fill=1.0, base=0,
                                            pattern=[[-1, P]], channel_multiplier=1).then_inc(pool_step, 1)
                nc.gpsimd.affine_select(out=mask_qk[:], in_=mask_qk[:], compare_op=ALU.is_ge, fill=MASKED, base=0,
                                        pattern=[[-1, P]], channel_multiplier=1).then_inc(pool_step, 1)
                nc.gpsimd.affine_select(out=mask_kq[:], in_=mask_kq[:], compare_op=ALU.is_ge, fill=MASKED, base=0,
                                        pattern=[[1, P]], channel_multiplier=-1).then_inc(pool_step, 1)

            @block.scalar
            def _(act):
                act.wait_ge(c_in, 16)
                nc.scalar.activation(silu[:], cc[:], ACT.Exp, scale=-1.0).then_inc(exp_done, 1)
                for c in range(NC_):
                    act.wait_ge(raw_in[c], 16)
                    nc.scalar.copy(wqkv[:, 0, c, :], raw[:, c, :]).then_inc(w_hi, 1)

            @block.vector
            def _(dve):
                dve.wait_ge(exp_done, 1)
                nc.vector.tensor_scalar_add(silu[:], silu[:], 1.0).then_inc(silu_step, 1)
                dve.wait_ge(silu_step, 1)
                nc.vector.reciprocal(silu[:], silu[:]).then_inc(silu_step, 1)
                dve.wait_ge(silu_step, 2)
                nc.vector.tensor_tensor(silu[:], silu[:], cc[:], ALU.mult).then_inc(silu_step, 1)
                for j in range(6):
                    dve.wait_ge(mod_mm, j + 1)
                    nc.vector.tensor_copy(rows[:, j * C:(j + 1) * C], psum[j][0:B, :]).then_inc(rows_done, 1)
                dve.wait_ge(rows_done, 6)
                for j in (1, 4):
                    nc.vector.tensor_scalar_add(rows[:, j * C:(j + 1) * C], rows[:, j * C:(j + 1) * C], 1.0)\
                        .then_inc(scale_done, 1)
                g = rows[:].rearrange("b (s j n) -> b s j n", s=2, j=3)[:, :, 2, :]
                nc.vector.tensor_scalar(sign[:], g, 0.0, 2.0, ALU.is_ge, ALU.mult).then_inc(gate_step, 1)
                nc.vector.scalar_tensor_tensor(out=flip[:], in0=g, scalar=-1.0, in1=g, op0=ALU.mult, op1=ALU.max)\
                    .then_inc(gate_step, 1)
                dve.wait_ge(gate_step, 2)
                nc.vector.tensor_scalar_add(sign[:], sign[:], -1.0).then_inc(gate_step, 1)
                nc.vector.tensor_scalar_max(flip[:], flip[:], GATE_FLOOR).then_inc(gate_step, 1)
                dve.wait_ge(gate_step, 4)
                nc.vector.tensor_tensor(gates[:], sign[:], flip[:], ALU.mult).then_inc(gate_step, 1)
                dve.wait_ge(col_mm, 1)
                nc.vector.tensor_copy(mod_cols[:].rearrange("p s j b -> p (s j b)"), psum[6][:, 0:4 * NC_ * B])
                for c in range(NC_):
                    dve.wait_ge(w_hi, c + 1)
                    nc.vector.tensor_tensor(wqkv[:, 1, c, :], raw[:, c, :], f32(wqkv[:, 0, c, :]), ALU.subtract)\
                        .then_inc(w_lo, 1)

            @block.tensor
            def _(pe):
                pe.wait_ge(silu_step, 3)
                for c in range(NC_):
                    pe.wait_ge(wm_in[c], 16)
                    for j in range(6):
                        mm = nc.tensor.matmul(psum[j][0:B, :], silu[:, c, :], wm[:, c, j * C:(j + 1) * C],
                                              start=(c == 0), stop=(c == NC_ - 1))
                        if c == NC_ - 1:
                            mm.then_inc(mod_mm, 1)
                pe.wait_ge(pool_step, 8)
                pe.wait_ge(scale_done, 2)
                for s in range(2):
                    for j in range(2):
                        for c in range(NC_):
                            at = ((s * 2 + j) * NC_ + c) * B
                            src = (3 * s + j) * C + c * P
                            mm = nc.tensor.transpose(psum[6][:, at:at + B], rows[:, src:src + P], ident[0:B, 0:B])
                mm.then_inc(col_mm, 1)


BY_QUERY = ((0, 0, 3, 0), (1, 0, 2, 0), (1, 0, 0, 384), (2, 1, 3, 0), (3, 1, 2, 0), (3, 1, 0, 384),
            (4, 0, 1, 0), (4, 1, 1, 256))
BY_KEY = tuple((u, h, NT - 1 - t, col) for u, h, t, col in BY_QUERY)
LO_ON_POOL = (0, 1, 3)
LO_ON_DVE = (2, 4)

TURN, QK, V = "turn", "qk", "v"


def qk(f):
    return [(QK, f, c) for c in range(NC_)]


def values(g, t):
    return [(V, g, t, i) for i in range(2)]


NEXT_FROM = 4
SEQUENCE = [(TURN, c) for c in range(NC_)] + qk(0) + qk(1) + qk(2) + qk(3) + values(0, 0) + values(0, 1) \
    + values(0, 2) + qk(4) + values(0, 3) + qk(5) + qk(6) + qk(7) \
    + values(1, 0) + values(1, 1) + values(1, 2) + values(1, 3)
PER_SLOT = (6, 6, 6, 6, 6, 7, 7, 8)
SLOT_ORDER = [(NEXT_FROM + i) % PAIRS for i in range(PAIRS)]
WORK = {p: [[] for _ in range(UNITS)] for p in SLOT_ORDER}
for i, p in enumerate(SLOT_ORDER):
    for j in range(PER_SLOT[i]):
        WORK[p][j * UNITS // PER_SLOT[i]].append(SEQUENCE[sum(PER_SLOT[:i]) + j])
assert sum(PER_SLOT) == len(SEQUENCE)


def last_item(item):
    return item[0] == TURN or item[-1] == (NC_ - 1 if item[0] == QK else 1)


def unit_of(item):
    return item if item[0] == TURN else item[:-1]


ORDER = [unit_of(i) for i in SEQUENCE if last_item(i)]
LIN = len(ORDER)
assert LIN % 2 == 0


def attention(nc, mem, x, wqkv, ident, mask_qk, mask_kq, ident_bf, mod_cols, attn_dram):
    xt = mem.sb("x_tiles", [P, NT, C])
    stats = mem.sb("bn_stats", [P, NT, 6])
    mean_var = mem.sb("mean_var", [P, NT, 2])
    var_eps = mem.sb("var_eps", [P, NT])
    rstd = mem.sb("rstd", [P, NT])
    minus_half = mem.sb("minus_half", [P, NT])
    mod_now = mem.sb("mod_now", [P, 2 * NC_])
    full = mem.sb("full", [P, 2, T])
    h = mem.sb("h_parts", [P, 2, NC_, T], F32R)
    qk_parts = mem.sb("qk_parts", [P, 2, 2, 2, T], F32R)
    stack = mem.sb("stack", [P, 2, H, T], F32R)
    v = mem.sb("v_parts", [P, NT, H, VW], BF16)
    row_max = mem.sb("row_max", [P, 2, 2, NT])
    neg_max = mem.sb("neg_max", [P, 2, 2, 2 * NT])
    max_rows = mem.sb("max_rows", [4 * NT, 2, P], F32R)
    prob = mem.sb("prob", [P, UNITS, 512])
    prob_hi = mem.sb("prob_hi", [P, 2, UNITS, 512], F16)
    prob_lo = mem.sb("prob_lo", [P, 2, UNITS, 512], F16)
    o_sum = mem.sb("o_sum", [P, 2, NT, 2, D])
    o_rcp = mem.sb("o_rcp", [P, 2, NT, 2, 1])
    o = mem.sb("o_rows", [P, 2, NT, P])
    score_bank, key_bank, lin_bank = mem.banks("score", 2), mem.banks("key_score", 2), mem.banks("lin", 2)
    o_bank, turn_bank = mem.banks("o_bank", 1)[0], mem.banks("turn", 1)[0]

    x_in = [mem.sem(f"x_in{t}") for t in range(NT)]
    aggr_done, var_ready, rstd_ready, x_norm, mod_ready = (
        mem.sem(n) for n in ("aggr_done", "var_ready", "rstd_ready", "x_norm", "mod_ready"))
    lin_done, lin_act, h_hi, lin_taken = (mem.sem(n) for n in ("lin_done", "lin_act", "h_hi", "lin_taken"))
    v_mid_ready, v_split = (mem.sem(n) for n in ("v_mid_ready", "v_split"))
    stack_in = [mem.sem(f"stack_in{g}") for g in range(GROUPS)]
    score_done, score_taken, max_hi, max_ready, turn_done, turn_taken = (
        mem.sem(n) for n in ("score_done", "score_taken", "max_hi", "max_ready", "turn_done", "turn_taken"))
    max_in = [mem.sem(f"max_in{p}") for p in range(PAIRS)]
    key_done, prob_ready, lo_dve, lo_pool, pv_done, o_taken, o_scaled, consts, consts_dve = (
        mem.sem(n) for n in ("key_done", "prob_ready", "lo_dve", "lo_pool", "pv_done", "o_taken", "o_scaled",
                             "consts", "consts_dve"))
    o_out = [mem.sem(f"o_out{g}") for g in range(2)]
    LIN_CREDITS, SCORE_CREDITS, KEY_CREDITS, O_CREDITS, SCALED_CREDITS, V_CREDITS = 2, 2, 2, 6, 2, 2
    STACK_DMAS = 3 * 4
    V_UNITS = 2 * NT

    def lin_no(n, unit):
        return LIN * n + ORDER.index(unit)

    def lin_bank_of(unit):
        return lin_bank[ORDER.index(unit) % 2]

    def v_no(n, g, t):
        return V_UNITS * n + NT * g + t

    def unit_no(b, p, u):
        return PAIRS * UNITS * b + UNITS * p + u

    def behind(b, p, lag, first):
        if p < lag:
            return None if first else (b - 1, p - lag + PAIRS)
        return (b, p - lag) if p - lag < PAIRS else None

    def work(b, p, u, more):
        if p >= PAIRS or (p >= NEXT_FROM and not more):
            return ()
        return [(b + 1 if p >= NEXT_FROM else b, item) for item in WORK[p][u]]

    def before_first():
        return [item for p in range(NEXT_FROM, PAIRS) for step in WORK[p] for item in step]

    TAIL = 4

    def over_batches(engine, slot):
        for p in range(PAIRS):
            slot(0, p, True, True)
        with engine.Fori(1, B - 1) as b:
            for p in range(PAIRS):
                slot(b, p, False, True)
        for p in range(PAIRS + TAIL):
            slot(B - 1, p, False, False)

    with nc.Block() as block:
        @block.sync
        def _(sp):
            def load_x(n):
                for t in range(NT):
                    sp.dma_start(xt[:, t, :], x[n, t * P:(t + 1) * P, :]).then_inc(x_in[t], 16)

            def load_stack(n, g):
                sp.wait_ge(lin_taken, LIN_CREDITS + lin_no(n, (QK, 2 * g + 1)) + 1)
                for block_row, (q_part, k_part) in enumerate(((0, 0), (1, 0), (0, 1))):
                    for j in range(4):
                        src = f32(qk_parts[32 * j:32 * j + 32, g % 2, :, :, :]).rearrange("p s l n -> p (s l) n")
                        step = 2 + k_part - q_part
                        sp.dma_start(f32(stack[32 * block_row:32 * block_row + 32, :, 4 * g + j, :]),
                                     src[:, q_part:q_part + step + 1:step, :]).then_inc(stack_in[g], 16)

            def after_item(n, item):
                if item[0] == QK and item[1] % 2 and last_item(item):
                    load_stack(n, item[1] // 2)

            for g in range(2):
                sp.sem_inc(o_out[g], 16)
            load_x(0)
            for item in before_first():
                after_item(0, item)

            def slot(b, p, first, more):
                if p == 0 and more:
                    wait_apart(sp, lin_done, lin_no(b, (TURN, NC_ - 1)) + 1, (o_out[0], 16))
                    load_x(b + 1)
                for u in range(UNITS):
                    for n, item in work(b, p, u, more):
                        after_item(n, item)
                    done = behind(b, p, 4, first)
                    if u == 1 and done and done[1] % 2:
                        g = done[1] // 2
                        wait_apart(sp, o_scaled, SCALED_CREDITS + PAIRS * done[0] + done[1] + 1, (o_out[0], 16))
                        cols = slice(g * P, (g + 1) * P)
                        sp.dma_start(attn_dram[done[0], :, cols].rearrange("(t p) n -> p t n", p=P),
                                     o[:, g % 2]).then_inc(o_out[g % 2], 16)

            over_batches(sp, slot)
            for g in range(2):
                sp.wait_ge(o_out[g], 16 + 16 * B * GROUPS // 2)

        @block.gpsimd
        def _(pool):
            nc.gpsimd.memset(minus_half[:], -0.5).then_inc(consts, 1)
            pool.wait_ge(consts, 1)
            pool.sem_inc(lo_pool, len(LO_ON_POOL))
            pool.sem_inc(o_scaled, SCALED_CREDITS)

            def inverse_deviation(n):
                pool.wait_ge(var_ready, n + 1)
                nc.gpsimd.tensor_tensor(rstd[:], var_eps[:], minus_half[:], ALU.pow).then_inc(rstd_ready, 1)

            inverse_deviation(0)

            def slot(b, p, first, more):
                for u in range(UNITS):
                    key = behind(b, p, 2, first)
                    if key and u in LO_ON_POOL:
                        pool.wait_ge(prob_ready, KEY_CREDITS + unit_no(*key, u) + 1)
                        nc.gpsimd.tensor_tensor(prob_lo[:, key[1] % 2, u, :], prob[:, u, :],
                                                prob_hi[:, key[1] % 2, u, :], ALU.subtract).then_inc(lo_pool, 1)
                    done = behind(b, p, 4, first)
                    if u == 0 and done:
                        n, q = done
                        pool.wait_ge(o_taken, O_CREDITS + H * n + 2 * q + 2)
                        g = q // 2
                        if q % 2 == 0:
                            pool.wait_ge(o_out[g % 2], 16 + 16 * (GROUPS // 2 * n + g // 2))
                        nc.gpsimd.tensor_tensor(
                            o[:, g % 2, :, q % 2 * 2 * D:(q % 2 + 1) * 2 * D].rearrange("p t (h d) -> p t h d", h=2),
                            o_sum[:, q % 2], o_rcp[:, q % 2].to_broadcast([P, NT, 2, D]), ALU.mult)\
                            .then_inc(o_scaled, 1)
                    if p == 2 and u == 4 and more:
                        inverse_deviation(b + 1)

            over_batches(pool, slot)

        @block.scalar
        def _(act):
            act.sem_inc(prob_ready, KEY_CREDITS)
            act.sem_inc(turn_taken, 1)

            def modulate(n, c):
                if c == 0:
                    act.wait_ge(mod_ready, n + 1)
                    act.wait_ge(v_split, V_CREDITS + V_UNITS * n)
                nc.scalar.activation(full[:, c % 2, :], lin_bank_of((TURN, c))[:], ACT.Identity,
                                     scale=mod_now[:, NC_ + c:NC_ + c + 1], bias=mod_now[:, c:c + 1])\
                    .then_inc(lin_act, 1)

            def qk_hi(f):
                nc.scalar.copy(qk_parts[:, f // 2 % 2, f % 2, 0, :], lin_bank_of((QK, f))[:]).then_inc(lin_act, 1)

            def v_high_parts(n, g, t):
                def heads(ap):
                    return ap.rearrange("p (h d) -> p h d", d=D)
                hs = slice(g * H // 2, (g + 1) * H // 2)
                nc.scalar.copy(v[:, t, hs, 0:D], heads(lin_bank_of((V, g, t))[:, 0:C // 2])).then_inc(lin_act, 1)
                act.wait_ge(lin_taken, LIN_CREDITS + lin_no(n, (V, g, t)) + 1)
                nc.scalar.copy(v[:, t, hs, D:2 * D], heads(full[:, ORDER.index((V, g, t)) % 2, 0:C // 2]))\
                    .then_inc(v_mid_ready, 1)

            def after_item(n, item, very_first=False):
                if not last_item(item):
                    return
                unit = unit_of(item)
                if item[0] == QK and item[1] % 2 == 0 and not (very_first and item[1] < 4):
                    g = item[1] // 2
                    act.wait_ge(stack_in[(g - 2) % GROUPS], 16 * STACK_DMAS * (n + 1 if g >= 2 else n))
                act.wait_ge(lin_done, lin_no(n, unit) + 1)
                if item[0] == TURN:
                    modulate(n, item[1])
                elif item[0] == QK:
                    qk_hi(item[1])
                else:
                    v_high_parts(n, item[1], item[2])

            for item in before_first():
                after_item(0, item, very_first=True)

            def slot(b, p, first, more):
                for u in range(UNITS):
                    key = behind(b, p, 2, first)
                    if key:
                        n, q = key
                        bank = key_bank[(UNITS * q + u) % 2]
                        act.wait_ge(key_done, unit_no(n, q, u) + 1)
                        if u == 0:
                            act.wait_ge(o_taken, O_CREDITS + H * n + 2 * (q - 2) + 2)
                        nc.scalar.activation(prob_hi[:, q % 2, u, :], bank[:], ACT.Exp, scale=SOFTMAX_SCALE,
                                             bias=P_SHIFT)
                        if u in LO_ON_DVE:
                            act.wait_ge(lo_dve, len(LO_ON_DVE) * (PAIRS * n + q) + LO_ON_DVE.index(u) + 1)
                        else:
                            act.wait_ge(lo_pool, len(LO_ON_POOL) * (PAIRS * n + q) + LO_ON_POOL.index(u) + 1)
                        nc.scalar.activation(prob[:, u, :], bank[:], ACT.Exp, scale=SOFTMAX_SCALE, bias=P_SHIFT)\
                            .then_inc(prob_ready, 1)
                    turned = behind(b, p, 1, first)
                    if u == 1 and turned:
                        n, q = turned
                        act.wait_ge(turn_done, PAIRS * n + q + 1)
                        nc.scalar.copy(max_rows[:, q % 2, :], turn_bank[0:4 * NT, 0:P]).then_inc(turn_taken, 1)
                        act.wait_ge(turn_taken, 1 + PAIRS * n + q + 1)
                        for part in range(2):
                            act.dma_start(
                                f32(stack[3 * D + part:3 * D + part + 1, 0, 2 * q:2 * q + 2, :]),
                                f32(max_rows[2 * NT * part:2 * NT * (part + 1), q % 2, :]))\
                                .then_inc(max_in[q], 16)
                    for n, item in work(b, p, u, more):
                        after_item(n, item)

            over_batches(act, slot)

        @block.vector
        def _(dve):
            nc.vector.memset(f32(stack[3 * D:3 * D + 2, 1, :, :]), 1.0).then_inc(consts_dve, 1)
            nc.vector.memset(v[:, :, :, 3 * D:VW], 1.0).then_inc(consts_dve, 1)
            dve.sem_inc(lin_taken, LIN_CREDITS)
            dve.sem_inc(v_split, V_CREDITS)
            dve.sem_inc(score_taken, SCORE_CREDITS)
            dve.sem_inc(lo_dve, len(LO_ON_DVE))
            dve.sem_inc(o_taken, O_CREDITS)

            def row_stats(n, tiles):
                for t in tiles:
                    dve.wait_ge(x_in[t], 16 * (n + 1))
                    nc.vector.bn_stats(stats[:, t, :], xt[:, t, :])
                dve.drain()
                for t in tiles:
                    nc.vector.bn_aggr(mean_var[:, t, :], stats[:, t, :]).then_inc(aggr_done, 1)

            def variance(n):
                dve.wait_ge(aggr_done, NT * (n + 1))
                nc.vector.tensor_scalar_add(var_eps[:], mean_var[:, :, 1], EPS).then_inc(var_ready, 1)
                nc.vector.tensor_copy(mod_now[:], mod_cols[:, 0, :, n]).then_inc(mod_ready, 1)

            def normalise(n):
                dve.wait_ge(rstd_ready, n + 1)
                for t in range(NT):
                    nc.vector.tensor_scalar(xt[:, t, :], xt[:, t, :], mean_var[:, t, 0:1], rstd[:, t:t + 1],
                                            ALU.subtract, ALU.mult).then_inc(x_norm, 1)

            def split_h(n, c):
                nc.vector.tensor_copy(h[:, 0, c, :], full[:, c % 2, :]).then_inc(h_hi, 1)
                dve.wait_ge(h_hi, NC_ * n + c + 1)
                nc.vector.tensor_tensor(h[:, 1, c, :], full[:, c % 2, :], f32(h[:, 0, c, :]), ALU.subtract)\
                    .then_inc(lin_taken, 1)

            def qk_lo(f):
                nc.vector.tensor_tensor(qk_parts[:, f // 2 % 2, f % 2, 1, :], lin_bank_of((QK, f))[:],
                                        f32(qk_parts[:, f // 2 % 2, f % 2, 0, :]), ALU.subtract).then_inc(lin_taken, 1)

            def v_low_part(n, g, t):
                def heads(ap):
                    return ap.rearrange("p (h d) -> p h d", d=D)
                hs = slice(g * H // 2, (g + 1) * H // 2)
                dve.wait_ge(v_split, V_CREDITS + v_no(n, g, t) - 1)
                rest = heads(full[:, ORDER.index((V, g, t)) % 2, 0:C // 2])
                nc.vector.tensor_tensor(rest, heads(lin_bank_of((V, g, t))[:, 0:C // 2]), v[:, t, hs, 0:D],
                                        ALU.subtract).then_inc(lin_taken, 1)
                dve.wait_ge(v_mid_ready, v_no(n, g, t) + 1)
                nc.vector.tensor_tensor(v[:, t, hs, 2 * D:3 * D], rest, v[:, t, hs, D:2 * D],
                                        ALU.subtract).then_inc(v_split, 1)

            def after_item(n, item):
                if not last_item(item):
                    return
                dve.wait_ge(lin_act, lin_no(n, unit_of(item)) + 1)
                if item[0] == TURN:
                    split_h(n, item[1])
                elif item[0] == QK:
                    qk_lo(item[1])
                else:
                    v_low_part(n, item[1], item[2])

            row_stats(0, range(NT))
            variance(0)
            normalise(0)
            for item in before_first():
                after_item(0, item)

            def gather_output(n, q, hh):
                dve.wait_ge(pv_done, H * n + 2 * q + hh + 1)
                if hh == 0:
                    dve.wait_ge(o_scaled, PAIRS * n + q + 1)
                parts = o_bank[:, 0:NT * VW].rearrange("p (t w) -> p t w", t=NT)
                nc.vector.tensor_reduce(o_sum[:, q % 2, :, hh, :],
                                        parts[:, :, 0:3 * D].rearrange("p t (k d) -> p t d k", k=3),
                                        axis=AX.X, op=ALU.add)
                nc.vector.reciprocal(o_rcp[:, q % 2, :, hh, :], parts[:, :, 3 * D:VW]).then_inc(o_taken, 1)

            def slot(b, p, first, more):
                for u in range(UNITS):
                    done = behind(b, p, 4, first)
                    if u == 0 and done:
                        gather_output(*done, 1)
                    if p < PAIRS:
                        bank = score_bank[(UNITS * p + u) % 2]
                        dve.wait_ge(score_done, unit_no(b, p, u) + 1)
                        if u == 4:
                            last = nc.vector.reduce_max(row_max[:, p % 2, :, 1],
                                                        bank[:].rearrange("p (h k) -> p h k", h=2), AX.X)
                        else:
                            for _, hh, t, col in (r for r in BY_QUERY if r[0] == u):
                                last = nc.vector.reduce_max(row_max[:, p % 2, hh, t:t + 1],
                                                            bank[:, col:col + P * (t + 1)], AX.X)
                        last.then_inc(score_taken, 1)
                    key = behind(b, p, 2, first)
                    if key and u in LO_ON_DVE:
                        dve.wait_ge(prob_ready, KEY_CREDITS + unit_no(*key, u) + 1)
                        nc.vector.tensor_tensor(prob_lo[:, key[1] % 2, u, :], prob[:, u, :],
                                                prob_hi[:, key[1] % 2, u, :], ALU.subtract).then_inc(lo_dve, 1)
                    weighted = behind(b, p, 3, first)
                    if u == 3 and weighted:
                        gather_output(*weighted, 0)
                    for n, item in work(b, p, u, more):
                        after_item(n, item)
                    if p < PAIRS and u == UNITS - 1:
                        dve.wait_ge(score_taken, SCORE_CREDITS + unit_no(b, p, UNITS))
                        peak = row_max[:, p % 2].rearrange("p h t -> p (h t)")
                        nc.vector.tensor_scalar_mul(neg_max[:, p % 2, 0, :].bitcast(F32R), peak, -1.0)\
                            .then_inc(max_hi, 1)
                        dve.wait_ge(max_hi, PAIRS * b + p + 1)
                        nc.vector.scalar_tensor_tensor(
                            out=neg_max[:, p % 2, 1, :].bitcast(F32R), in0=peak, scalar=-1.0,
                            in1=neg_max[:, p % 2, 0, :], op0=ALU.mult, op1=ALU.subtract).then_inc(max_ready, 1)
                    if more and (p, u) == (1, 1):
                        row_stats(b + 1, (0, 1))
                    if more and (p, u) == (1, 3):
                        row_stats(b + 1, (2, 3))
                        variance(b + 1)
                    if more and (p, u) == (3, 0):
                        normalise(b + 1)

            over_batches(dve, slot)

        @block.tensor
        def _(pe):
            def turn(n, c):
                if c == 0:
                    pe.wait_ge(x_norm, NT * (n + 1))
                bank = lin_bank_of((TURN, c))
                for t in range(NT):
                    mm = nc.tensor.transpose(bank[:, t * P:(t + 1) * P], xt[:, t, c * P:(c + 1) * P], ident[:])
                return mm

            def qk_terms(n, f, c):
                if f == 0:
                    pe.wait_ge(lin_taken, LIN_CREDITS + lin_no(n, (TURN, c)) + 1)
                at = (f % 2) * C + (f // 2) * P
                for k, (wl, hl) in enumerate(TERMS):
                    mm = nc.tensor.matmul(lin_bank_of((QK, f))[:], wqkv[:, wl, c, at:at + P], h[:, hl, c, :],
                                          start=(c == 0 and k == 0), stop=(c == NC_ - 1 and k == 2))
                return mm

            def v_terms(g, t, i):
                at = 2 * C + g * C // 2
                for c in (2 * i, 2 * i + 1):
                    for k, (wl, hl) in enumerate(TERMS):
                        mm = nc.tensor.matmul(lin_bank_of((V, g, t))[:, 0:C // 2], h[:, hl, c, t * P:(t + 1) * P],
                                              wqkv[:, wl, c, at:at + C // 2],
                                              start=(c == 0 and k == 0), stop=(c == NC_ - 1 and k == 2))
                return mm

            def do_item(n, item):
                if item[0] == TURN or item[-1] == 0:
                    pe.wait_ge(lin_taken, lin_no(n, unit_of(item)) + 1)
                if item[0] == TURN:
                    mm = turn(n, item[1])
                elif item[0] == QK:
                    mm = qk_terms(n, item[1], item[2])
                else:
                    mm = v_terms(*item[1:])
                if last_item(item):
                    mm.then_inc(lin_done, 1)

            pe.wait_ge(consts_dve, 2)
            for item in before_first():
                do_item(0, item)

            def scores_by_query(b, p, u):
                bank = score_bank[(UNITS * p + u) % 2]
                if u == 0:
                    pe.wait_ge(stack_in[p // 2], 16 * STACK_DMAS * (b + 1))
                pe.wait_ge(score_taken, unit_no(b, p, u) + 1)
                for _, hh, t, col in (r for r in BY_QUERY if r[0] == u):
                    head, n = 2 * p + hh, P * (t + 1)
                    nc.tensor.matmul(bank[:, col:col + n], stack[0:3 * D, 0, head, t * P:(t + 1) * P],
                                     stack[0:3 * D, 1, head, 0:n], start=True, stop=False)
                    mm = nc.tensor.matmul(bank[:, col + n - P:col + n], ident_bf[:], mask_qk[:],
                                          start=False, stop=True)
                mm.then_inc(score_done, 1)

            def scores_by_key(b, p, u):
                bank = key_bank[(UNITS * p + u) % 2]
                if u == 0:
                    pe.wait_ge(max_in[p], 32 * (b + 1))
                pe.wait_ge(prob_ready, unit_no(b, p, u) + 1)
                for _, hh, t, col in (r for r in BY_KEY if r[0] == u):
                    head, n = 2 * p + hh, T - P * t
                    nc.tensor.matmul(bank[:, col:col + n], stack[0:3 * D + 2, 1, head, t * P:(t + 1) * P],
                                     stack[0:3 * D + 2, 0, head, t * P:T], start=True, stop=False)
                    mm = nc.tensor.matmul(bank[:, col:col + P], ident_bf[:], mask_kq[:], start=False, stop=True)
                mm.then_inc(key_done, 1)

            def weighted_values(b, p, hh):
                head = 2 * p + hh
                if hh == 0:
                    pe.wait_ge(lo_dve, len(LO_ON_DVE) * (PAIRS * b + p + 2))
                    pe.wait_ge(lo_pool, len(LO_ON_POOL) * (PAIRS * b + p + 2))
                    if p % (PAIRS // 2) == 0:
                        pe.wait_ge(v_split, V_CREDITS + V_UNITS * b + NT * (p // (PAIRS // 2) + 1))
                pe.wait_ge(o_taken, O_CREDITS + H * b + head)
                place = {t: (u, col) for u, h2, t, col in BY_KEY if h2 == hh}
                for i in range(NT):
                    for j in range(i + 1):
                        u, col = place[j]
                        at = col + P * (i - j)
                        for part in (prob_hi, prob_lo):
                            mm = nc.tensor.matmul(o_bank[:, i * VW:(i + 1) * VW], part[:, p % 2, u, at:at + P],
                                                  v[:, j, head, :], start=(j == 0 and part is prob_hi),
                                                  stop=(j == i and part is prob_lo))
                mm.then_inc(pv_done, 1)

            def slot(b, p, first, more):
                for u in range(UNITS):
                    if p < PAIRS:
                        scores_by_query(b, p, u)
                    key = behind(b, p, 2, first)
                    if key:
                        scores_by_key(*key, u)
                    turned = behind(b, p, 1, first)
                    if u == 1 and turned:
                        n, q = turned
                        pe.wait_ge(max_ready, PAIRS * n + q + 1)
                        pe.wait_ge(turn_taken, PAIRS * n + q + 1)
                        nc.tensor.transpose(turn_bank[0:4 * NT, 0:P],
                                            neg_max[:, q % 2, :, :].rearrange("p l m -> p (l m)"), ident[:])\
                            .then_inc(turn_done, 1)
                    for n, item in work(b, p, u, more):
                        do_item(n, item)
                    weighted = behind(b, p, 3, first)
                    if weighted and u in (2, 4):
                        weighted_values(*weighted, u // 2 - 1)

            over_batches(pe, slot)


def load_mlp_weights(nc, weights):
    SLOTS = 6
    with ExitStack() as ctx:
        mem = Memory(nc, ctx)
        raw = mem.sb("w_raw", [P, SLOTS, F])
        raw_in = [mem.sem(f"w_raw_in{i}") for i in range(SLOTS)]
        hi_done, lo_done = mem.sem("w_hi_done"), mem.sem("w_lo_done")
        strips = [(src, dst, c) for src, dst in weights for c in range(src.shape[0] // P)]

        with nc.Block() as block:
            @block.sync
            def _(sp):
                for i, (src, dst, c) in enumerate(strips):
                    if i >= SLOTS:
                        sp.wait_ge(lo_done, i - SLOTS + 1)
                    sp.dma_start(raw[:, i % SLOTS, 0:src.shape[1]], src[c * P:(c + 1) * P, :])\
                        .then_inc(raw_in[i % SLOTS], 16)

            @block.scalar
            def _(act):
                for i, (src, dst, c) in enumerate(strips):
                    act.wait_ge(raw_in[i % SLOTS], 16 * (i // SLOTS + 1))
                    nc.scalar.copy(dst[:, 0, c, :], raw[:, i % SLOTS, 0:src.shape[1]]).then_inc(hi_done, 1)

            @block.vector
            def _(dve):
                for i, (src, dst, c) in enumerate(strips):
                    dve.wait_ge(hi_done, i + 1)
                    nc.vector.tensor_tensor(dst[:, 1, c, :], raw[:, i % SLOTS, 0:src.shape[1]], f32(dst[:, 0, c, :]),
                                            ALU.subtract).then_inc(lo_done, 1)


CH = 256
CT = CH // P
HALVES = T // CH
FB = NC_ + 2 * NF
TB = NC_ + 2 * CT
PROJ_AFTER = 2
NORM_AFTER = 4


def mlp(nc, mem, x, attn_dram, gate_dram, wproj, w1, w2, w3, b1_c, b2_c, b3, ident, mod_cols, out):
    ga = mem.sb("gate_attn", [P, C])
    gb = mem.sb("gate_mlp", [P, C])
    b3_rows = mem.sb("b3_rows", [P, C])
    b1_cols = mem.sb("b1_cols", [P, NF])
    b2_cols = mem.sb("b2_cols", [P, NF])
    mod_now = mem.sb("mlp_mod_now", [P, 2 * NC_])
    at = mem.sb("attn_tiles", [P, CT, C])
    xt = mem.sb("res_tiles", [P, HALVES, CT, C])
    a = mem.sb("turned", [P, 2, NC_, CH], F32R)
    y1 = mem.sb("y1", [P, 2, NF, CH], F32R)
    y2 = mem.sb("y2", [P, 2, NF, CH], F32R)
    full = mem.sb("mlp_full", [P, 2, CH])
    gated = mem.sb("gated", [P, C])
    stats = mem.sb("mlp_stats", [P, CT, 6])
    mean_var = mem.sb("mlp_mean_var", [P, CT, 2])
    var_eps = mem.sb("mlp_var_eps", [P, CT])
    rstd = mem.sb("mlp_rstd", [P, CT])
    minus_half = mem.sb("mlp_minus_half", [P, CT])
    fbank, tbank = mem.banks("feature", 4), mem.banks("token", 4)

    const_in, ga_in, gb_in = mem.sem("const_in"), mem.sem("ga_in"), mem.sem("gb_in")
    at_in = mem.sem("at_in")
    res_in = [mem.sem(f"res_in{h}") for h in range(HALVES)]
    out_done = [mem.sem(f"out_done{h}") for h in range(HALVES)]
    (f_done, f_act, f_hi, f_split, t_done, t_act, t_taken, gate_step, x2_ready, stats_done, aggr_done, var_ready,
     rstd_ready, x_norm, mod_ready, out_step, out_ready, consts) = (mem.sem(n) for n in (
         "f_done", "f_act", "f_hi", "f_split", "t_done", "t_act", "t_taken", "gate_step", "x2_ready",
         "mlp_stats_done", "mlp_aggr_done", "mlp_var_ready", "mlp_rstd_ready", "mlp_x_norm", "mlp_mod_ready",
         "out_step", "out_ready", "mlp_consts"))
    F_CREDITS, FULL_CREDITS, T_CREDITS = 4, 2, 4

    def rows_no(k, c):
        return FB * k + c

    def layer_no(k, layer, f):
        return FB * k + NC_ + NF * (layer - 1) + f

    def turned_no(k, c):
        return TB * k + c if k_is_first(k) else TB * k - CT + c

    def k_is_first(k):
        return isinstance(k, int) and k == 0

    def proj_no(k, t):
        return turned_no(k, NC_) + t

    def last_no(k, t, more):
        return TB * k + NC_ + CT + (NC_ + CT if more else 0) + t

    def over_chunks(engine, body):
        with engine.Fori(0, B - 1) as b:
            for half in range(HALVES):
                body(HALVES * b + half, b, half, True)
        for half in range(HALVES):
            body(HALVES * (B - 1) + half, B - 1, half, half < HALVES - 1)

    def following(b, half):
        return (b, half + 1) if half < HALVES - 1 else (b + 1, 0)

    def fbank_of(k_even_no):
        return fbank[k_even_no % 4]

    def tiles(dram, b, half):
        return dram[b, half * CH:(half + 1) * CH, :].rearrange("(t p) n -> p t n", p=P)

    with nc.Block() as block:
        @block.sync
        def _(sp):
            def load_gate(tile, b, which, sem):
                sp.dma_start(tile[:], gate_dram[b:b + 1, which * C:(which + 1) * C].to_broadcast([P, C])
                             if isinstance(b, int) else
                             gate_dram[bass.ds(b, 1), which * C:(which + 1) * C].to_broadcast([P, C])).then_inc(sem, 16)

            def load_attn(b, half):
                sp.dma_start(at[:], tiles(attn_dram, b, half)).then_inc(at_in, 16)

            def load_x(b, half):
                sp.dma_start(xt[:, half], tiles(x, b, half)).then_inc(res_in[half], 16)

            held = (out_done[0], 16)
            load_attn(0, 0)
            load_x(0, 0)
            load_gate(ga, 0, 0, ga_in)
            load_gate(gb, 0, 1, gb_in)
            sp.dma_start(b1_cols[:], b1_c).then_inc(const_in, 16)
            sp.dma_start(b2_cols[:], b2_c).then_inc(const_in, 16)
            sp.dma_start(b3_rows[:], b3.to_broadcast([P, C])).then_inc(const_in, 16)

            def chunk(k, b, half, more):
                nb, nh = following(b, half)
                if more:
                    wait_apart(sp, f_done, rows_no(k, NC_), held)
                    load_attn(nb, nh)
                    wait_apart(sp, out_done[nh], 16 * (b + half + 1), held)
                    load_x(nb, nh)
                    if nh == 0:
                        wait_apart(sp, t_taken, T_CREDITS + proj_no(k, CT), held)
                        load_gate(ga, nb, 0, ga_in)
                if more and nh == 0:
                    sp.wait_ge(out_ready, CT * (k + 1))
                    load_gate(gb, nb, 1, gb_in)

            over_chunks(sp, chunk)

        @block.gpsimd
        def _(pool):
            nc.gpsimd.memset(minus_half[:], -0.5).then_inc(consts, 1)
            pool.wait_ge(consts, 1)

            def inverse_deviation(k):
                pool.wait_ge(var_ready, k + 1)
                nc.gpsimd.tensor_tensor(rstd[:], var_eps[:], minus_half[:], ALU.pow).then_inc(rstd_ready, 1)

            inverse_deviation(0)

            def chunk(k, b, half, more):
                if more:
                    inverse_deviation(k + 1)

            over_chunks(pool, chunk)

        @block.scalar
        def _(act):
            act.sem_inc(f_act, F_CREDITS)
            for half in range(HALVES):
                act.sem_inc(out_done[half], 16)

            def turned_hi(k, c, at_no):
                act.wait_ge(t_done, turned_no(k, c) + 1)
                nc.scalar.copy(a[:, 0, c, :], tbank[at_no % 4][:, 0:CH]).then_inc(t_act, 1)

            def modulate(k, b, c):
                act.wait_ge(f_done, rows_no(k, c) + 1)
                act.wait_ge(f_split, rows_no(k, c) + 1)
                if c == 0:
                    act.wait_ge(mod_ready, b + 1)
                nc.scalar.activation(full[:, c % 2, :], fbank[c % 4][:, 0:CH], ACT.Identity,
                                     scale=mod_now[:, NC_ + c:NC_ + c + 1], bias=mod_now[:, c:c + 1])\
                    .then_inc(f_act, 1)

            def hidden(k, layer, f):
                act.wait_ge(f_done, layer_no(k, layer, f) + 1)
                act.wait_ge(f_split, layer_no(k, layer, f) + 1)
                bias = (b1_cols, b2_cols)[layer - 1]
                nc.scalar.activation(full[:, f % 2, :], fbank[f % 4][:, 0:CH], ACT.Relu, bias=bias[:, f:f + 1])\
                    .then_inc(f_act, 1)

            act.wait_ge(const_in, 48)
            for c in range(NC_):
                turned_hi(0, c, c)
            for c in range(NC_):
                modulate(0, 0, c)

            def chunk(k, b, half, more):
                nb, nh = following(b, half)
                for f in range(NF):
                    hidden(k, 1, f)
                if more:
                    for c in range(NC_):
                        turned_hi(k + 1, c, turned_no(1, c))
                for f in range(NF):
                    hidden(k, 2, f)
                if more:
                    for c in range(NC_):
                        modulate(k + 1, nb, c)
                act.wait_ge(out_ready, CT * (k + 1))
                act.dma_start(tiles(out, b, half), xt[:, half]).then_inc(out_done[half], 16)

            over_chunks(act, chunk)
            for half in range(HALVES):
                act.wait_ge(out_done[half], 16 * (B + 1))

        @block.vector
        def _(dve):
            dve.sem_inc(f_split, FULL_CREDITS)
            dve.sem_inc(t_taken, T_CREDITS)

            def turned_lo(k, c, at_no):
                dve.wait_ge(t_act, NC_ * k + c + 1)
                nc.vector.tensor_tensor(a[:, 1, c, :], tbank[at_no % 4][:, 0:CH], f32(a[:, 0, c, :]), ALU.subtract)\
                    .then_inc(t_taken, 1)

            def split(dst, c, number, ring):
                dve.wait_ge(f_act, F_CREDITS + number + 1)
                nc.vector.tensor_copy(dst[:, 0, c, :], full[:, ring, :]).then_inc(f_hi, 1)
                dve.wait_ge(f_hi, number + 1)
                nc.vector.tensor_tensor(dst[:, 1, c, :], full[:, ring, :], f32(dst[:, 0, c, :]), ALU.subtract)\
                    .then_inc(f_split, 1)

            def add_attention(k, b, half, t, at_no):
                dve.wait_ge(t_done, proj_no(k, t) + 1)
                if half == 0 and t == 0:
                    dve.wait_ge(ga_in, 16 * (b + 1))
                nc.vector.tensor_tensor(gated[:], tbank[at_no % 4][:], ga[:], ALU.mult).then_inc(t_taken, 1)
                dve.wait_ge(t_taken, T_CREDITS + proj_no(k, t) + 1)
                dve.wait_ge(res_in[half], 16 * (b + 1))
                nc.vector.tensor_tensor(xt[:, half, t, :], xt[:, half, t, :], gated[:], ALU.add).then_inc(x2_ready, 1)
                dve.wait_ge(x2_ready, CT * k + t + 1)
                nc.vector.bn_stats(stats[:, t, :], xt[:, half, t, :]).then_inc(stats_done, 1)
                dve.drain()
                nc.vector.bn_aggr(mean_var[:, t, :], stats[:, t, :]).then_inc(aggr_done, 1)

            def variance(k):
                dve.wait_ge(aggr_done, CT * (k + 1))
                nc.vector.tensor_scalar_add(var_eps[:], mean_var[:, :, 1], EPS).then_inc(var_ready, 1)

            def normalise(k, b, half):
                dve.wait_ge(rstd_ready, k + 1)
                for t in range(CT):
                    nc.vector.tensor_scalar(at[:, t, :], xt[:, half, t, :], mean_var[:, t, 0:1], rstd[:, t:t + 1],
                                            ALU.subtract, ALU.mult).then_inc(x_norm, 1)
                if half == 0:
                    nc.vector.tensor_copy(mod_now[:], mod_cols[:, 1, :, b]).then_inc(mod_ready, 1)

            def finish(k, b, half, t, more):
                dve.wait_ge(t_done, last_no(k, t, more) + 1)
                if half == 0 and t == 0:
                    dve.wait_ge(gb_in, 16 * (b + 1))
                if t:
                    dve.wait_ge(out_ready, CT * k + t)
                nc.vector.tensor_tensor(gated[:], tbank[last_no(0, t, more) % 4][:], b3_rows[:], ALU.add).then_inc(t_taken, 1)
                dve.wait_ge(t_taken, T_CREDITS + last_no(k, t, more) + 1)
                nc.vector.tensor_tensor(gated[:], gated[:], gb[:], ALU.mult).then_inc(out_step, 1)
                dve.wait_ge(out_step, CT * k + t + 1)
                nc.vector.tensor_tensor(xt[:, half, t, :], xt[:, half, t, :], gated[:], ALU.add).then_inc(out_ready, 1)

            dve.wait_ge(const_in, 48)
            for c in range(NC_):
                turned_lo(0, c, c)
            for t in range(CT):
                add_attention(0, 0, 0, t, NC_ + t)
            variance(0)
            normalise(0, 0, 0)
            for c in range(NC_):
                split(a, c, rows_no(0, c), c % 2)

            def chunk(k, b, half, more):
                nb, nh = following(b, half)
                for f in range(NF):
                    split(y1, f, layer_no(k, 1, f), f % 2)
                if more:
                    for c in range(NC_):
                        turned_lo(k + 1, c, turned_no(1, c))
                for f in range(NF):
                    split(y2, f, layer_no(k, 2, f), f % 2)
                    if more and f == PROJ_AFTER - 1:
                        for t in range(CT):
                            add_attention(k + 1, nb, nh, t, proj_no(1, t))
                        variance(k + 1)
                    if more and f == NORM_AFTER - 1:
                        normalise(k + 1, nb, nh)
                if more:
                    for c in range(NC_):
                        split(a, c, rows_no(k + 1, c), c % 2)
                for t in range(CT):
                    finish(k, b, half, t, more)

            over_chunks(dve, chunk)

        @block.tensor
        def _(pe):
            def turn_attention(k, c, at_no):
                if c == 0:
                    pe.wait_ge(at_in, 16 * (k + 1))
                pe.wait_ge(t_taken, turned_no(k, c) + 1)
                for t in range(CT):
                    mm = nc.tensor.transpose(tbank[at_no % 4][:, t * P:(t + 1) * P], at[:, t, c * P:(c + 1) * P],
                                             ident[:])
                mm.then_inc(t_done, 1)

            def turn_rows(k, c):
                if c == 0:
                    pe.wait_ge(x_norm, CT * (k + 1))
                pe.wait_ge(f_act, rows_no(k, c) + 1)
                for t in range(CT):
                    mm = nc.tensor.transpose(fbank[c % 4][:, t * P:(t + 1) * P], at[:, t, c * P:(c + 1) * P], ident[:])
                mm.then_inc(f_done, 1)

            def token_rows(weights, data, chunks, t, bank, number, ready):
                pe.wait_ge(t_taken, number + 1)
                for c in range(chunks):
                    if t == 0:
                        ready(c)
                    for i, (wl, dl) in enumerate(TERMS):
                        mm = nc.tensor.matmul(bank[:], data[:, dl, c, t * P:(t + 1) * P], weights[:, wl, c, :],
                                              start=(c == 0 and i == 0), stop=(c == chunks - 1 and i == 2))
                mm.then_inc(t_done, 1)

            def project(k, t, at_no):
                token_rows(wproj, a, NC_, t, tbank[at_no % 4], proj_no(k, t),
                           lambda c: pe.wait_ge(t_taken, T_CREDITS + turned_no(k, c) + 1))

            def last_layer(k, t, more):
                token_rows(w3, y2, NF, t, tbank[last_no(0, t, more) % 4], last_no(k, t, more),
                           lambda c: pe.wait_ge(f_split, FULL_CREDITS + layer_no(k, 2, c) + 1))

            def hidden(k, layer, f):
                weights, data, chunks = ((w1, a, NC_), (w2, y1, NF))[layer - 1]
                pe.wait_ge(f_act, layer_no(k, layer, f) + 1)
                for c in range(chunks):
                    if f == 0:
                        pe.wait_ge(f_split, FULL_CREDITS + 1 + (rows_no(k, c) if layer == 1 else layer_no(k, 1, c)))
                    for i, (wl, dl) in enumerate(TERMS):
                        mm = nc.tensor.matmul(fbank[f % 4][:, 0:CH], weights[:, wl, c, f * P:(f + 1) * P],
                                              data[:, dl, c, :], start=(c == 0 and i == 0),
                                              stop=(c == chunks - 1 and i == 2))
                mm.then_inc(f_done, 1)

            for c in range(NC_):
                turn_attention(0, c, c)
            for t in range(CT):
                project(0, t, NC_ + t)
            for c in range(NC_):
                turn_rows(0, c)

            def chunk(k, b, half, more):
                for f in range(NF):
                    hidden(k, 1, f)
                if more:
                    for c in range(NC_):
                        turn_attention(k + 1, c, turned_no(1, c))
                for f in range(NF):
                    hidden(k, 2, f)
                    if more and f == PROJ_AFTER - 1:
                        for t in range(CT):
                            project(k + 1, t, proj_no(1, t))
                if more:
                    for c in range(NC_):
                        turn_rows(k + 1, c)
                for t in range(CT):
                    last_layer(k, t, more)

            over_chunks(pe, chunk)


def kernel(L0_attn_x, L0_attn_W_attn, L0_attn_W_proj, L0_ffn_W1, L0_ffn_b1, L0_ffn_W2, L0_ffn_b2, L0_ffn_W3,
           L0_ffn_b3, L0_c, L0_wmod):
    import numpy as np
    import concourse.bacc as bacc
    from concourse.bass_utils import run_bass_kernel_spmd

    arrays = {
        "x": L0_attn_x, "wqkv_t": np.asarray(L0_attn_W_attn).T, "wproj_t": np.asarray(L0_attn_W_proj).T,
        "w1_t": np.asarray(L0_ffn_W1).T, "b1_c": np.asarray(L0_ffn_b1).reshape(NF, P).T,
        "w2_t": np.asarray(L0_ffn_W2).T, "b2_c": np.asarray(L0_ffn_b2).reshape(NF, P).T,
        "w3_t": np.asarray(L0_ffn_W3).T, "b3": np.asarray(L0_ffn_b3).reshape(1, C),
        "c_t": np.asarray(L0_c).T, "wmod": L0_wmod,
    }
    arrays = {k: np.ascontiguousarray(a) for k, a in arrays.items()}
    nc = bacc.Bacc("TRN2", target_bir_lowering=False, num_devices=1)
    ins = {k: nc.dram_tensor(k, a.shape, mybir.dt.from_np(a.dtype), kind="ExternalInput").ap()
           for k, a in arrays.items()}
    attn_dram = nc.dram_tensor("attn_dram", (B, T, C), F32, kind="Internal").ap()
    gate_dram = nc.dram_tensor("gate_dram", (B, 2 * C), F32, kind="Internal").ap()
    out = nc.dram_tensor("out", (B, T, C), F32, kind="ExternalOutput").ap()
    build(nc, attn_dram=attn_dram, gate_dram=gate_dram, out=out, **ins)
    result = run_bass_kernel_spmd(nc, [arrays], core_ids=[0])
    return result.results[0]["out"]
```

```python
from contextlib import ExitStack

import concourse.bass as bass
from concourse import mybir

F32 = mybir.dt.float32
F32R = mybir.dt.float32r
F16 = mybir.dt.float16
BF16 = mybir.dt.bfloat16
ALU = mybir.AluOpType
ACT = mybir.ActivationFunctionType
AX = mybir.AxisListType

P = 128
B, T, C = 8, 512, 512
H, D = 16, 32
F = 1024
NC_ = C // P
NF = F // P
NT = T // P
PAIRS = H // 2
GROUPS = H // 4
UNITS = 5
SOFTMAX_SCALE = float(D) ** -0.5
P_SHIFT = 12 * 0.6931471805599453
MASKED = -1e30
EPS = 1e-5
GATE_FLOOR = 0.25
VW = 3 * D + 1
TERMS = ((0, 0), (0, 1), (1, 0))


def f32(ap):
    return ap.bitcast(F32)


def wait_apart(engine, sem, value, held):
    engine.wait_ge(*held)
    engine.wait_ge(sem, value)


class Memory:

    def __init__(self, nc, ctx):
        self.nc, self.ctx = nc, ctx

    def sb(self, name, shape, dt=F32):
        return self.ctx.enter_context(self.nc.sbuf_tensor(name, shape, dt))

    def banks(self, name, n):
        return [self.ctx.enter_context(self.nc.psum_tensor(f"{name}{i}", [P, 512], F32)) for i in range(n)]

    def sem(self, name):
        return self.ctx.enter_context(self.nc.semaphore(name))


def build(nc, x, wqkv_t, wproj_t, w1_t, b1_c, w2_t, b2_c, w3_t, b3, c_t, wmod, attn_dram, gate_dram, out):
    with ExitStack() as ctx:
        mem = Memory(nc, ctx)
        ident = mem.sb("ident", [P, P])
        mod_cols = mem.sb("mod_cols", [P, 2, 2 * NC_, B])
        with ExitStack() as attention_ctx:
            amem = Memory(nc, attention_ctx)
            wqkv = amem.sb("wqkv", [P, 2, NC_, 3 * C], F32R)
            mask_qk = amem.sb("mask_qk", [P, P], BF16)
            mask_kq = amem.sb("mask_kq", [P, P], BF16)
            ident_bf = amem.sb("ident_bf", [P, P], BF16)
            setup(nc, ident, mod_cols, wqkv, mask_qk, mask_kq, ident_bf, wqkv_t, c_t, wmod, gate_dram)
            attention(nc, amem, x, wqkv, ident, mask_qk, mask_kq, ident_bf, mod_cols, attn_dram)
        with ExitStack() as mlp_ctx:
            mmem = Memory(nc, mlp_ctx)
            wproj = mmem.sb("wproj", [P, 2, NC_, C], F32R)
            w1 = mmem.sb("w1", [P, 2, NC_, F], F32R)
            w2 = mmem.sb("w2", [P, 2, NF, F], F32R)
            w3 = mmem.sb("w3", [P, 2, NF, C], F32R)
            weights = ((wproj_t, wproj), (w1_t, w1), (w2_t, w2), (w3_t, w3))
            mlp(nc, mmem, x, attn_dram, gate_dram, weights, b1_c, b2_c, b3, ident, mod_cols, out)


def setup(nc, ident, mod_cols, wqkv, mask_qk, mask_kq, ident_bf, wqkv_t, c_t, wmod, gate_dram):
    SIX = 6 * C
    GATES = (2, 5)
    with ExitStack() as ctx:
        mem = Memory(nc, ctx)
        raw = mem.sb("wqkv_raw", [P, NC_, 3 * C])
        wm = mem.sb("wmod_sb", [P, NC_, SIX])
        cc = mem.sb("c_sb", [P, NC_, B])
        silu = mem.sb("silu", [P, NC_, B])
        rows = mem.sb("mod_rows", [B, SIX])
        flip = mem.sb("gate_abs", [B, 2, C])
        sign = mem.sb("gate_sign", [B, 2, C])
        gates = mem.sb("gates", [B, 2, C])
        psum = mem.banks("mod_psum", 7)
        c_in, gates_out = mem.sem("c_in"), mem.sem("gates_out")
        raw_in = [mem.sem(f"raw_in{c}") for c in range(NC_)]
        wm_in = [mem.sem(f"wm_in{c}") for c in range(NC_)]
        pool_step, exp_done, silu_step, mod_mm, rows_done = (
            mem.sem(n) for n in ("pool_step", "exp_done", "silu_step", "mod_mm", "rows_done"))
        gate_in, gate_step, col_mm, w_hi, w_lo = (
            mem.sem(n) for n in ("gate_in", "gate_step", "col_mm", "w_hi", "w_lo"))

        with nc.Block() as block:
            @block.sync
            def _(sp):
                sp.dma_start(cc[:], c_t.rearrange("(c p) b -> p c b", p=P)).then_inc(c_in, 16)
                for c in range(NC_):
                    sp.dma_start(raw[:, c, :], wqkv_t[c * P:(c + 1) * P, :]).then_inc(raw_in[c], 16)
                for c in range(NC_):
                    sp.dma_start(wm[:, c, :], wmod[c * P:(c + 1) * P, :]).then_inc(wm_in[c], 16)
                sp.wait_ge(gate_step, 5)
                sp.dma_start(gate_dram.rearrange("b (g n) -> b g n", g=2), gates[:]).then_inc(gates_out, 16)
                sp.wait_ge(gates_out, 16)

            @block.gpsimd
            def _(pool):
                nc.gpsimd.memset(ident[:], 0.0).then_inc(pool_step, 1)
                nc.gpsimd.memset(ident_bf[:], 0.0).then_inc(pool_step, 1)
                nc.gpsimd.memset(mask_qk[:], 0.0).then_inc(pool_step, 1)
                nc.gpsimd.memset(mask_kq[:], 0.0).then_inc(pool_step, 1)
                pool.wait_ge(pool_step, 4)
                for m in (ident, ident_bf):
                    nc.gpsimd.affine_select(out=m[:], in_=m[:], compare_op=ALU.not_equal, fill=1.0, base=0,
                                            pattern=[[-1, P]], channel_multiplier=1).then_inc(pool_step, 1)
                nc.gpsimd.affine_select(out=mask_qk[:], in_=mask_qk[:], compare_op=ALU.is_ge, fill=MASKED, base=0,
                                        pattern=[[-1, P]], channel_multiplier=1).then_inc(pool_step, 1)
                nc.gpsimd.affine_select(out=mask_kq[:], in_=mask_kq[:], compare_op=ALU.is_ge, fill=MASKED, base=0,
                                        pattern=[[1, P]], channel_multiplier=-1).then_inc(pool_step, 1)

            @block.scalar
            def _(act):
                act.wait_ge(c_in, 16)
                nc.scalar.activation(silu[:], cc[:], ACT.Exp, scale=-1.0).then_inc(exp_done, 1)
                for c in range(NC_):
                    act.wait_ge(raw_in[c], 16)
                    nc.scalar.copy(wqkv[:, 0, c, :], raw[:, c, :]).then_inc(w_hi, 1)
                for j, plus in ((0, 0.0), (1, 1.0), (3, 0.0), (4, 1.0)):
                    act.wait_ge(mod_mm, j + 1)
                    nc.scalar.activation(rows[:, j * C:(j + 1) * C], psum[j][0:B, :], ACT.Identity, bias=plus)\
                        .then_inc(rows_done, 1)

            @block.vector
            def _(dve):
                dve.wait_ge(exp_done, 1)
                nc.vector.tensor_scalar_add(silu[:], silu[:], 1.0).then_inc(silu_step, 1)
                dve.wait_ge(silu_step, 1)
                nc.vector.reciprocal(silu[:], silu[:]).then_inc(silu_step, 1)
                dve.wait_ge(silu_step, 2)
                nc.vector.tensor_tensor(silu[:], silu[:], cc[:], ALU.mult).then_inc(silu_step, 1)
                for c in range(NC_):
                    dve.wait_ge(w_hi, c + 1)
                    nc.vector.tensor_tensor(wqkv[:, 1, c, :], raw[:, c, :], f32(wqkv[:, 0, c, :]), ALU.subtract)\
                        .then_inc(w_lo, 1)
                for j in GATES:
                    dve.wait_ge(mod_mm, j + 1)
                    nc.vector.tensor_copy(rows[:, j * C:(j + 1) * C], psum[j][0:B, :]).then_inc(gate_in, 1)
                dve.wait_ge(gate_in, 2)
                g = rows[:].rearrange("b (s j n) -> b s j n", s=2, j=3)[:, :, 2, :]
                nc.vector.tensor_scalar(sign[:], g, 0.0, 2.0, ALU.is_ge, ALU.mult).then_inc(gate_step, 1)
                nc.vector.scalar_tensor_tensor(out=flip[:], in0=g, scalar=-1.0, in1=g, op0=ALU.mult, op1=ALU.max)\
                    .then_inc(gate_step, 1)
                dve.wait_ge(gate_step, 2)
                nc.vector.tensor_scalar_add(sign[:], sign[:], -1.0).then_inc(gate_step, 1)
                nc.vector.tensor_scalar_max(flip[:], flip[:], GATE_FLOOR).then_inc(gate_step, 1)
                dve.wait_ge(gate_step, 4)
                nc.vector.tensor_tensor(gates[:], sign[:], flip[:], ALU.mult).then_inc(gate_step, 1)
                dve.wait_ge(col_mm, 1)
                nc.vector.tensor_copy(mod_cols[:].rearrange("p s j b -> p (s j b)"), psum[6][:, 0:4 * NC_ * B])

            @block.tensor
            def _(pe):
                pe.wait_ge(silu_step, 3)
                for c in range(NC_):
                    pe.wait_ge(wm_in[c], 16)
                    for j in range(6):
                        mm = nc.tensor.matmul(psum[j][0:B, :], silu[:, c, :], wm[:, c, j * C:(j + 1) * C],
                                              start=(c == 0), stop=(c == NC_ - 1))
                        if c == NC_ - 1:
                            mm.then_inc(mod_mm, 1)
                pe.wait_ge(pool_step, 8)
                pe.wait_ge(rows_done, 4)
                for s in range(2):
                    for j in range(2):
                        for c in range(NC_):
                            at = ((s * 2 + j) * NC_ + c) * B
                            src = (3 * s + j) * C + c * P
                            mm = nc.tensor.transpose(psum[6][:, at:at + B], rows[:, src:src + P], ident[0:B, 0:B])
                mm.then_inc(col_mm, 1)


BY_QUERY = ((0, 0, 3, 0), (1, 0, 2, 0), (1, 0, 0, 384), (2, 1, 3, 0), (3, 1, 2, 0), (3, 1, 0, 384),
            (4, 0, 1, 0), (4, 1, 1, 256))
BY_KEY = ((0, 0, 0, 0), (1, 0, 3, 0), (1, 0, 1, 128), (2, 1, 0, 0), (3, 1, 3, 0), (3, 1, 1, 128),
          (4, 0, 2, 0), (4, 1, 2, 256))
LO_ON_POOL = (0, 1, 3, 4)
LO_ON_DVE = (2,)


def diagonals(bank, u, by_key):
    first = {t: col if by_key else col + P * t for u2, _, t, col in (BY_KEY if by_key else BY_QUERY) if u2 == u}
    if u in (0, 2):
        at = list(first.values())[0]
        return bank[:, at:at + P]
    if u == 4:
        at = 0 if by_key else P
        return bank[:].rearrange("p (h n) -> p h n", h=2)[:, :, at:at + P]
    at = min(first.values())
    return bank[:, at:at + 2 * P].rearrange("p (h n) -> p h n", h=2)


def mask_for(mask, u):
    return mask[:] if u in (0, 2) else mask[:].unsqueeze(1).broadcast_to([P, 2, P])

TURN, QK, V = "turn", "qk", "v"


def qk(f):
    return [(QK, f, c) for c in range(NC_)]


def values(g, t):
    return [(V, g, t, i) for i in range(2)]


NEXT_FROM = 4
SEQUENCE = [(TURN, c) for c in range(NC_)] + qk(0) + qk(1) + qk(2) + qk(3) + values(0, 0) + values(0, 1) \
    + values(0, 2) + qk(4) + values(0, 3) + qk(5) + qk(6) + qk(7) \
    + values(1, 0) + values(1, 1) + values(1, 2) + values(1, 3)
PER_SLOT = (6, 6, 6, 6, 6, 7, 7, 8)
SLOT_ORDER = [(NEXT_FROM + i) % PAIRS for i in range(PAIRS)]
WORK = {p: [[] for _ in range(UNITS)] for p in SLOT_ORDER}
for i, p in enumerate(SLOT_ORDER):
    for j in range(PER_SLOT[i]):
        WORK[p][j * UNITS // PER_SLOT[i] if i else min(j, UNITS - 1)].append(SEQUENCE[sum(PER_SLOT[:i]) + j])
assert sum(PER_SLOT) == len(SEQUENCE)


def last_item(item):
    return item[0] == TURN or item[-1] == (NC_ - 1 if item[0] == QK else 1)


def unit_of(item):
    return item if item[0] == TURN else item[:-1]


ORDER = [unit_of(i) for i in SEQUENCE if last_item(i)]
LIN = len(ORDER)
assert LIN % 2 == 0


def attention(nc, mem, x, wqkv, ident, mask_qk, mask_kq, ident_bf, mod_cols, attn_dram):
    xt = mem.sb("x_tiles", [P, NT, C])
    stats = mem.sb("bn_stats", [P, NT, 6])
    mean_var = mem.sb("mean_var", [P, NT, 2])
    var_eps = mem.sb("var_eps", [P, NT])
    rstd = mem.sb("rstd", [P, NT])
    minus_half = mem.sb("minus_half", [P, NT])
    mod_now = mem.sb("mod_now", [P, 2 * NC_])
    full = mem.sb("full", [P, 2, T])
    h = mem.sb("h_parts", [P, 2, NC_, T], F32R)
    qk_parts = mem.sb("qk_parts", [P, 2, 2, 2, T], F32R)
    stack = mem.sb("stack", [P, 2, H, T], F32R)
    v = mem.sb("v_parts", [P, NT, H, VW], BF16)
    row_max = mem.sb("row_max", [P, 2, 2, NT])
    neg_max = mem.sb("neg_max", [P, 2, 2, 2 * NT])
    max_rows = mem.sb("max_rows", [4 * NT, 2, P], F32R)
    prob = mem.sb("prob", [P, UNITS, 512])
    prob_hi = mem.sb("prob_hi", [P, 2, UNITS, 512], F16)
    prob_lo = mem.sb("prob_lo", [P, 2, UNITS, 512], F16)
    o_sum = mem.sb("o_sum", [P, 2, NT, 2, D])
    o_rcp = mem.sb("o_rcp", [P, 2, NT, 2, 1])
    o = mem.sb("o_rows", [P, 2, NT, P])
    score_bank, key_bank, lin_bank = mem.banks("score", 2), mem.banks("key_score", 2), mem.banks("lin", 2)
    o_bank, turn_bank = mem.banks("o_bank", 1)[0], mem.banks("turn", 1)[0]

    x_in = [mem.sem(f"x_in{t}") for t in range(NT)]
    aggr_done, var_ready, rstd_ready, x_norm, mod_ready = (
        mem.sem(n) for n in ("aggr_done", "var_ready", "rstd_ready", "x_norm", "mod_ready"))
    lin_done, lin_act, h_hi, lin_taken = (mem.sem(n) for n in ("lin_done", "lin_act", "h_hi", "lin_taken"))
    v_mid_ready, v_split = (mem.sem(n) for n in ("v_mid_ready", "v_split"))
    stack_in = [mem.sem(f"stack_in{g}") for g in range(GROUPS)]
    score_done, score_taken, max_hi, max_ready, turn_done, turn_taken = (
        mem.sem(n) for n in ("score_done", "score_taken", "max_hi", "max_ready", "turn_done", "turn_taken"))
    max_in = [mem.sem(f"max_in{p}") for p in range(PAIRS)]
    key_done, prob_ready, lo_dve, lo_pool, pv_done, o_taken, o_scaled, consts, ones_ready = (
        mem.sem(n) for n in ("key_done", "prob_ready", "lo_dve", "lo_pool", "pv_done", "o_taken", "o_scaled",
                             "consts", "ones_ready"))
    o_out = [mem.sem(f"o_out{g}") for g in range(2)]
    LIN_CREDITS, SCORE_CREDITS, KEY_CREDITS, PV_CREDITS, SCALED_CREDITS, V_CREDITS = 2, 2, 2, 4, 2, 2
    O_CREDITS = 1
    STACK_DMAS = 3 * 4
    V_UNITS = 2 * NT

    def lin_no(n, unit):
        return LIN * n + ORDER.index(unit)

    def lin_bank_of(unit):
        return lin_bank[ORDER.index(unit) % 2]

    def v_no(n, g, t):
        return V_UNITS * n + NT * g + t

    def unit_no(b, p, u):
        return PAIRS * UNITS * b + UNITS * p + u

    def behind(b, p, lag, first):
        if p < lag:
            return None if first else (b - 1, p - lag + PAIRS)
        return (b, p - lag) if p - lag < PAIRS else None

    def work(b, p, u, more):
        if p >= PAIRS or (p >= NEXT_FROM and not more):
            return ()
        return [(b + 1 if p >= NEXT_FROM else b, item) for item in WORK[p][u]]

    def before_first():
        return [item for p in range(NEXT_FROM, PAIRS) for step in WORK[p] for item in step]

    TAIL = 4

    def over_batches(engine, slot):
        for p in range(PAIRS):
            slot(0, p, True, True)
        with engine.Fori(1, B - 1) as b:
            for p in range(PAIRS):
                slot(b, p, False, True)
        for p in range(PAIRS + TAIL):
            slot(B - 1, p, False, False)

    with nc.Block() as block:
        @block.sync
        def _(sp):
            def load_x(n):
                for t in range(NT):
                    sp.dma_start(xt[:, t, :], x[n, t * P:(t + 1) * P, :]).then_inc(x_in[t], 16)

            def load_stack(n, g):
                sp.wait_ge(lin_taken, LIN_CREDITS + lin_no(n, (QK, 2 * g + 1)) + 1)
                for block_row, (q_part, k_part) in enumerate(((0, 0), (1, 0), (0, 1))):
                    for j in range(4):
                        src = f32(qk_parts[32 * j:32 * j + 32, g % 2, :, :, :]).rearrange("p s l n -> p (s l) n")
                        step = 2 + k_part - q_part
                        sp.dma_start(f32(stack[32 * block_row:32 * block_row + 32, :, 4 * g + j, :]),
                                     src[:, q_part:q_part + step + 1:step, :]).then_inc(stack_in[g], 16)

            def after_item(n, item):
                if item[0] == QK and item[1] % 2 and last_item(item):
                    load_stack(n, item[1] // 2)

            for g in range(2):
                sp.sem_inc(o_out[g], 16)
            load_x(0)
            for item in before_first():
                after_item(0, item)

            def slot(b, p, first, more):
                if p == 0 and more:
                    wait_apart(sp, lin_done, lin_no(b, (TURN, NC_ - 1)) + 1, (o_out[0], 16))
                    load_x(b + 1)
                for u in range(UNITS):
                    for n, item in work(b, p, u, more):
                        after_item(n, item)
                    done = behind(b, p, 4, first)
                    if u == 1 and done and done[1] % 2:
                        g = done[1] // 2
                        wait_apart(sp, o_scaled, SCALED_CREDITS + PAIRS * done[0] + done[1] + 1, (o_out[0], 16))
                        cols = slice(g * P, (g + 1) * P)
                        sp.dma_start(attn_dram[done[0], :, cols].rearrange("(t p) n -> p t n", p=P),
                                     o[:, g % 2]).then_inc(o_out[g % 2], 16)

            over_batches(sp, slot)
            for g in range(2):
                sp.wait_ge(o_out[g], 16 + 16 * B * GROUPS // 2)

        @block.gpsimd
        def _(pool):
            nc.gpsimd.memset(minus_half[:], -0.5).then_inc(consts, 1)
            pool.wait_ge(consts, 1)
            pool.sem_inc(lo_pool, len(LO_ON_POOL))
            pool.sem_inc(o_scaled, SCALED_CREDITS)

            def inverse_deviation(n):
                pool.wait_ge(var_ready, n + 1)
                nc.gpsimd.tensor_tensor(rstd[:], var_eps[:], minus_half[:], ALU.pow).then_inc(rstd_ready, 1)

            inverse_deviation(0)
            pool.wait_ge(rstd_ready, 1)
            nc.gpsimd.memset(f32(stack[3 * D:3 * D + 2, 1, :, :]), 1.0).then_inc(ones_ready, 1)
            pool.wait_ge(ones_ready, 1)
            nc.gpsimd.memset(v[:, :, :, 3 * D:VW], 1.0).then_inc(ones_ready, 1)
            pool.wait_ge(ones_ready, 2)

            def slot(b, p, first, more):
                for u in range(UNITS):
                    key = behind(b, p, 2, first)
                    if key and u in LO_ON_POOL:
                        pool.wait_ge(prob_ready, KEY_CREDITS + unit_no(*key, u) + 1)
                        nc.gpsimd.tensor_tensor(prob_lo[:, key[1] % 2, u, :], prob[:, u, :],
                                                prob_hi[:, key[1] % 2, u, :], ALU.subtract).then_inc(lo_pool, 1)
                    done = behind(b, p, 4, first)
                    if u == 0 and done:
                        n, q = done
                        pool.wait_ge(o_taken, O_CREDITS + H * n + 2 * q + 2)
                        g = q // 2
                        if q % 2 == 0:
                            pool.wait_ge(o_out[g % 2], 16 + 16 * (GROUPS // 2 * n + g // 2))
                        nc.gpsimd.tensor_tensor(
                            o[:, g % 2, :, q % 2 * 2 * D:(q % 2 + 1) * 2 * D].rearrange("p t (h d) -> p t h d", h=2),
                            o_sum[:, q % 2], o_rcp[:, q % 2].to_broadcast([P, NT, 2, D]), ALU.mult)\
                            .then_inc(o_scaled, 1)
                    if p == 2 and u == 4 and more:
                        inverse_deviation(b + 1)

            over_batches(pool, slot)

        @block.scalar
        def _(act):
            act.sem_inc(prob_ready, KEY_CREDITS)
            act.sem_inc(turn_taken, 1)

            def modulate(n, c):
                if c == 0:
                    act.wait_ge(mod_ready, n + 1)
                    act.wait_ge(v_split, V_CREDITS + V_UNITS * n)
                nc.scalar.activation(full[:, c % 2, :], lin_bank_of((TURN, c))[:], ACT.Identity,
                                     scale=mod_now[:, NC_ + c:NC_ + c + 1], bias=mod_now[:, c:c + 1])\
                    .then_inc(lin_act, 1)

            def qk_hi(f):
                nc.scalar.copy(qk_parts[:, f // 2 % 2, f % 2, 0, :], lin_bank_of((QK, f))[:]).then_inc(lin_act, 1)

            def v_high_parts(n, g, t):
                def heads(ap):
                    return ap.rearrange("p (h d) -> p h d", d=D)
                hs = slice(g * H // 2, (g + 1) * H // 2)
                nc.scalar.copy(v[:, t, hs, D:2 * D], heads(lin_bank_of((V, g, t))[:, 0:C // 2])).then_inc(lin_act, 1)
                act.wait_ge(lin_taken, LIN_CREDITS + lin_no(n, (V, g, t)) + 1)
                nc.scalar.copy(v[:, t, hs, 2 * D:3 * D], heads(full[:, ORDER.index((V, g, t)) % 2, 0:C // 2]))\
                    .then_inc(v_mid_ready, 1)

            def after_item(n, item, very_first=False):
                if not last_item(item):
                    return
                unit = unit_of(item)
                if item[0] == QK and item[1] % 2 == 0 and not (very_first and item[1] < 4):
                    g = item[1] // 2
                    act.wait_ge(stack_in[(g - 2) % GROUPS], 16 * STACK_DMAS * (n + 1 if g >= 2 else n))
                act.wait_ge(lin_done, lin_no(n, unit) + 1)
                if item[0] == TURN:
                    modulate(n, item[1])
                elif item[0] == QK:
                    qk_hi(item[1])
                else:
                    v_high_parts(n, item[1], item[2])

            for item in before_first():
                after_item(0, item, very_first=True)

            def slot(b, p, first, more):
                for u in range(UNITS):
                    key = behind(b, p, 2, first)
                    if key:
                        n, q = key
                        bank = key_bank[(UNITS * q + u) % 2]
                        act.wait_ge(key_done, unit_no(n, q, u) + 1)
                        if u == 0:
                            act.wait_ge(pv_done, PV_CREDITS + H * n + 2 * (q - 2) + 2)
                        nc.scalar.activation(prob_hi[:, q % 2, u, :], bank[:], ACT.Exp, scale=SOFTMAX_SCALE,
                                             bias=P_SHIFT)
                        if u in LO_ON_DVE:
                            act.wait_ge(lo_dve, len(LO_ON_DVE) * (PAIRS * n + q) + LO_ON_DVE.index(u) + 1)
                        else:
                            act.wait_ge(lo_pool, len(LO_ON_POOL) * (PAIRS * n + q) + LO_ON_POOL.index(u) + 1)
                        nc.scalar.activation(prob[:, u, :], bank[:], ACT.Exp, scale=SOFTMAX_SCALE, bias=P_SHIFT)\
                            .then_inc(prob_ready, 1)
                    turned = behind(b, p, 1, first)
                    if u == 1 and turned:
                        n, q = turned
                        act.wait_ge(turn_done, PAIRS * n + q + 1)
                        nc.scalar.copy(max_rows[:, q % 2, :], turn_bank[0:4 * NT, 0:P]).then_inc(turn_taken, 1)
                        act.wait_ge(turn_taken, 1 + PAIRS * n + q + 1)
                        for part in range(2):
                            act.dma_start(
                                f32(stack[3 * D + part:3 * D + part + 1, 0, 2 * q:2 * q + 2, :]),
                                f32(max_rows[2 * NT * part:2 * NT * (part + 1), q % 2, :]))\
                                .then_inc(max_in[q], 16)
                    for n, item in work(b, p, u, more):
                        after_item(n, item)

            over_batches(act, slot)

        @block.vector
        def _(dve):
            dve.sem_inc(lin_taken, LIN_CREDITS)
            dve.sem_inc(v_split, V_CREDITS)
            dve.sem_inc(score_taken, SCORE_CREDITS)
            dve.sem_inc(lo_dve, len(LO_ON_DVE))
            dve.sem_inc(o_taken, O_CREDITS)

            def row_stats(n, tiles):
                for t in tiles:
                    dve.wait_ge(x_in[t], 16 * (n + 1))
                    nc.vector.bn_stats(stats[:, t, :], xt[:, t, :])
                dve.drain()
                for t in tiles:
                    nc.vector.bn_aggr(mean_var[:, t, :], stats[:, t, :]).then_inc(aggr_done, 1)

            def variance(n):
                dve.wait_ge(aggr_done, NT * (n + 1))
                nc.vector.tensor_scalar_add(var_eps[:], mean_var[:, :, 1], EPS).then_inc(var_ready, 1)
                nc.vector.tensor_copy(mod_now[:], mod_cols[:, 0, :, n]).then_inc(mod_ready, 1)

            def normalise(n):
                dve.wait_ge(rstd_ready, n + 1)
                for t in range(NT):
                    nc.vector.tensor_scalar(xt[:, t, :], xt[:, t, :], mean_var[:, t, 0:1], rstd[:, t:t + 1],
                                            ALU.subtract, ALU.mult).then_inc(x_norm, 1)

            def split_h(n, c):
                nc.vector.tensor_copy(h[:, 0, c, :], full[:, c % 2, :]).then_inc(h_hi, 1)
                dve.wait_ge(h_hi, NC_ * n + c + 1)
                nc.vector.tensor_tensor(h[:, 1, c, :], full[:, c % 2, :], f32(h[:, 0, c, :]), ALU.subtract)\
                    .then_inc(lin_taken, 1)

            def qk_lo(f):
                nc.vector.tensor_tensor(qk_parts[:, f // 2 % 2, f % 2, 1, :], lin_bank_of((QK, f))[:],
                                        f32(qk_parts[:, f // 2 % 2, f % 2, 0, :]), ALU.subtract).then_inc(lin_taken, 1)

            def heads(ap):
                return ap.rearrange("p (h d) -> p h d", d=D)

            def v_rest(n, g, t):
                hs = slice(g * H // 2, (g + 1) * H // 2)
                dve.wait_ge(v_split, V_CREDITS + v_no(n, g, t) - 1)
                rest = heads(full[:, ORDER.index((V, g, t)) % 2, 0:C // 2])
                nc.vector.tensor_tensor(rest, heads(lin_bank_of((V, g, t))[:, 0:C // 2]), v[:, t, hs, D:2 * D],
                                        ALU.subtract).then_inc(lin_taken, 1)

            def v_lowest(n, g, t):
                hs = slice(g * H // 2, (g + 1) * H // 2)
                rest = heads(full[:, ORDER.index((V, g, t)) % 2, 0:C // 2])
                dve.wait_ge(v_mid_ready, v_no(n, g, t) + 1)
                nc.vector.tensor_tensor(v[:, t, hs, 0:D], rest, v[:, t, hs, 2 * D:3 * D],
                                        ALU.subtract).then_inc(v_split, 1)

            def after_item(n, item):
                if not last_item(item):
                    return
                dve.wait_ge(lin_act, lin_no(n, unit_of(item)) + 1)
                if item[0] == TURN:
                    split_h(n, item[1])
                elif item[0] == QK:
                    qk_lo(item[1])
                else:
                    v_rest(n, item[1], item[2])

            def step_after_item(n, item):
                if item[0] == V and last_item(item):
                    v_lowest(n, item[1], item[2])

            row_stats(0, range(NT))
            variance(0)
            normalise(0)
            for item in before_first():
                after_item(0, item)
                step_after_item(0, item)

            def gather_output(n, q, hh):
                dve.wait_ge(pv_done, PV_CREDITS + H * n + 2 * q + hh + 1)
                if hh == 0:
                    dve.wait_ge(o_scaled, PAIRS * n + q + 1)
                parts = o_bank[:, 0:NT * VW].rearrange("p (t w) -> p t w", t=NT)
                nc.vector.tensor_reduce(o_sum[:, q % 2, :, hh, :],
                                        parts[:, :, 0:3 * D].rearrange("p t (k d) -> p t d k", k=3),
                                        axis=AX.X, op=ALU.add)
                nc.vector.reciprocal(o_rcp[:, q % 2, :, hh, :], parts[:, :, 3 * D:VW]).then_inc(o_taken, 1)

            def slot(b, p, first, more):
                for u in range(UNITS):
                    weighted = behind(b, p, 3, first)
                    if weighted and u in (2, 4):
                        gather_output(*weighted, u // 2 - 1)
                    if p < PAIRS:
                        bank = score_bank[(UNITS * p + u) % 2]
                        dve.wait_ge(score_done, unit_no(b, p, u) + 1)
                        if u == 4:
                            last = nc.vector.reduce_max(row_max[:, p % 2, :, 1],
                                                        bank[:].rearrange("p (h k) -> p h k", h=2), AX.X)
                        else:
                            for _, hh, t, col in (r for r in BY_QUERY if r[0] == u):
                                last = nc.vector.reduce_max(row_max[:, p % 2, hh, t:t + 1],
                                                            bank[:, col:col + P * (t + 1)], AX.X)
                        last.then_inc(score_taken, 1)
                    if not (first and p == u == 0):
                        earlier = (work(b, p, u - 1, more) if u else work(b, p - 1, UNITS - 1, more) if p
                                   else [(b, item) for item in WORK[PAIRS - 1][UNITS - 1]])
                        for n, item in earlier:
                            step_after_item(n, item)
                    key = behind(b, p, 2, first)
                    if key and u in LO_ON_DVE:
                        dve.wait_ge(prob_ready, KEY_CREDITS + unit_no(*key, u) + 1)
                        nc.vector.tensor_tensor(prob_lo[:, key[1] % 2, u, :], prob[:, u, :],
                                                prob_hi[:, key[1] % 2, u, :], ALU.subtract).then_inc(lo_dve, 1)
                    for n, item in work(b, p, u, more):
                        after_item(n, item)
                    if p < PAIRS and u == UNITS - 1:
                        dve.wait_ge(score_taken, SCORE_CREDITS + unit_no(b, p, UNITS))
                        peak = row_max[:, p % 2].rearrange("p h t -> p (h t)")
                        nc.vector.tensor_scalar_mul(neg_max[:, p % 2, 0, :].bitcast(F32R), peak, -1.0)\
                            .then_inc(max_hi, 1)
                        dve.wait_ge(max_hi, PAIRS * b + p + 1)
                        nc.vector.scalar_tensor_tensor(
                            out=neg_max[:, p % 2, 1, :].bitcast(F32R), in0=peak, scalar=-1.0,
                            in1=neg_max[:, p % 2, 0, :], op0=ALU.mult, op1=ALU.subtract).then_inc(max_ready, 1)
                    if more and (p, u) == (1, 1):
                        row_stats(b + 1, (0, 1))
                    if more and (p, u) == (1, 3):
                        row_stats(b + 1, (2, 3))
                        variance(b + 1)
                    if more and (p, u) == (3, 0):
                        normalise(b + 1)

            over_batches(dve, slot)

        @block.tensor
        def _(pe):
            def turn(n, c):
                if c == 0:
                    pe.wait_ge(x_norm, NT * (n + 1))
                bank = lin_bank_of((TURN, c))
                for t in range(NT):
                    mm = nc.tensor.transpose(bank[:, t * P:(t + 1) * P], xt[:, t, c * P:(c + 1) * P], ident[:])
                return mm

            def qk_terms(n, f, c):
                if f == 0:
                    pe.wait_ge(lin_taken, LIN_CREDITS + lin_no(n, (TURN, c)) + 1)
                at = (f % 2) * C + (f // 2) * P
                for k, (wl, hl) in enumerate(TERMS):
                    mm = nc.tensor.matmul(lin_bank_of((QK, f))[:], wqkv[:, wl, c, at:at + P], h[:, hl, c, :],
                                          start=(c == 0 and k == 0), stop=(c == NC_ - 1 and k == 2))
                return mm

            def v_terms(g, t, i):
                at = 2 * C + g * C // 2
                for c in (2 * i, 2 * i + 1):
                    for k, (wl, hl) in enumerate(TERMS):
                        mm = nc.tensor.matmul(lin_bank_of((V, g, t))[:, 0:C // 2], h[:, hl, c, t * P:(t + 1) * P],
                                              wqkv[:, wl, c, at:at + C // 2],
                                              start=(c == 0 and k == 0), stop=(c == NC_ - 1 and k == 2))
                return mm

            def do_item(n, item):
                if item[0] == TURN or item[-1] == 0:
                    pe.wait_ge(lin_taken, lin_no(n, unit_of(item)) + 1)
                if item[0] == TURN:
                    mm = turn(n, item[1])
                elif item[0] == QK:
                    mm = qk_terms(n, item[1], item[2])
                else:
                    mm = v_terms(*item[1:])
                if last_item(item):
                    mm.then_inc(lin_done, 1)

            pe.sem_inc(pv_done, PV_CREDITS)
            for item in before_first():
                do_item(0, item)
            pe.wait_ge(ones_ready, 2)

            def scores_by_query(b, p, u):
                bank = score_bank[(UNITS * p + u) % 2]
                if u == 0:
                    pe.wait_ge(stack_in[p // 2], 16 * STACK_DMAS * (b + 1))
                pe.wait_ge(score_taken, unit_no(b, p, u) + 1)
                for i, (_, hh, t, col) in enumerate(r for r in BY_QUERY if r[0] == u):
                    head, n = 2 * p + hh, P * (t + 1)
                    nc.tensor.matmul(bank[:, col:col + n], stack[0:3 * D, 0, head, t * P:(t + 1) * P],
                                     stack[0:3 * D, 1, head, 0:n], start=(i == 0), stop=False)
                nc.tensor.matmul(diagonals(bank, u, False), ident_bf[:], mask_for(mask_qk, u),
                                 start=False, stop=True).then_inc(score_done, 1)

            def scores_by_key(b, p, u):
                bank = key_bank[(UNITS * p + u) % 2]
                if u == 0:
                    pe.wait_ge(max_in[p], 32 * (b + 1))
                pe.wait_ge(prob_ready, unit_no(b, p, u) + 1)
                for i, (_, hh, t, col) in enumerate(r for r in BY_KEY if r[0] == u):
                    head, n = 2 * p + hh, T - P * t
                    nc.tensor.matmul(bank[:, col:col + n], stack[0:3 * D + 2, 1, head, t * P:(t + 1) * P],
                                     stack[0:3 * D + 2, 0, head, t * P:T], start=(i == 0), stop=False)
                nc.tensor.matmul(diagonals(bank, u, True), ident_bf[:], mask_for(mask_kq, u),
                                 start=False, stop=True).then_inc(key_done, 1)

            def weighted_values(b, p, hh):
                head = 2 * p + hh
                if hh == 0:
                    pe.wait_ge(lo_dve, len(LO_ON_DVE) * (PAIRS * b + p + 2))
                    pe.wait_ge(lo_pool, len(LO_ON_POOL) * (PAIRS * b + p + 2))
                    if p % (PAIRS // 2) == 0:
                        pe.wait_ge(v_split, V_CREDITS + V_UNITS * b + NT * (p // (PAIRS // 2) + 1))
                pe.wait_ge(o_taken, O_CREDITS + H * b + head)
                place = {t: (u, col) for u, h2, t, col in BY_KEY if h2 == hh}
                for i in range(NT):
                    for j in range(i + 1):
                        u, col = place[j]
                        at = col + P * (i - j)
                        for part, low in ((prob_hi, 0), (prob_lo, D)):
                            mm = nc.tensor.matmul(o_bank[:, i * VW + low:(i + 1) * VW], part[:, p % 2, u, at:at + P],
                                                  v[:, j, head, low:VW], start=(j == 0 and part is prob_hi),
                                                  stop=(j == i and part is prob_lo))
                mm.then_inc(pv_done, 1)

            def slot(b, p, first, more):
                for u in range(UNITS):
                    if p < PAIRS:
                        scores_by_query(b, p, u)
                    key = behind(b, p, 2, first)
                    if key:
                        scores_by_key(*key, u)
                    turned = behind(b, p, 1, first)
                    if u == 1 and turned:
                        n, q = turned
                        pe.wait_ge(max_ready, PAIRS * n + q + 1)
                        pe.wait_ge(turn_taken, PAIRS * n + q + 1)
                        nc.tensor.transpose(turn_bank[0:4 * NT, 0:P],
                                            neg_max[:, q % 2, :, :].rearrange("p l m -> p (l m)"), ident[:])\
                            .then_inc(turn_done, 1)
                    for n, item in work(b, p, u, more):
                        do_item(n, item)
                    weighted = behind(b, p, 3, first)
                    if weighted and u in (1, 3):
                        weighted_values(*weighted, u // 2)

            over_batches(pe, slot)


CH = 256
CT = CH // P
HALVES = T // CH
FB = NC_ + 2 * NF
TB = NC_ + 2 * CT
PROJ_AFTER = 2
NORM_AFTER = 4


def mlp(nc, mem, x, attn_dram, gate_dram, weights, b1_c, b2_c, b3, ident, mod_cols, out):
    (_, wproj), (_, w1), (_, w2), (_, w3) = weights
    ga = mem.sb("gate_attn", [P, C])
    gb = mem.sb("gate_mlp", [P, C])
    b3_rows = mem.sb("b3_rows", [P, C])
    b1_cols = mem.sb("b1_cols", [P, NF])
    b2_cols = mem.sb("b2_cols", [P, NF])
    mod_now = mem.sb("mlp_mod_now", [P, 2 * NC_])
    at = mem.sb("attn_tiles", [P, CT, C])
    xt = mem.sb("res_tiles", [P, HALVES, CT, C])
    a = mem.sb("turned", [P, 2, NC_, CH], F32R)
    y1 = mem.sb("y1", [P, 2, NF, CH], F32R)
    RING_WORDS = 2 * NF * CH
    with ExitStack() as ring_ctx:
        ring = Memory(nc, ring_ctx).sb("w_ring", [P, RING_WORDS])
    y2 = mem.sb("y2", [P, 2, NF, CH], F32R)
    full = mem.sb("mlp_full", [P, 2, CH])
    gated = mem.sb("gated", [P, C])
    stats = mem.sb("mlp_stats", [P, CT, 6])
    mean_var = mem.sb("mlp_mean_var", [P, CT, 2])
    var_eps = mem.sb("mlp_var_eps", [P, CT])
    rstd = mem.sb("mlp_rstd", [P, CT])
    minus_half = mem.sb("mlp_minus_half", [P, CT])
    fbank, tbank = mem.banks("feature", 4), mem.banks("token", 4)

    strips = [(src, dst, c) for src, dst in weights for c in range(src.shape[0] // P)]
    strip_at = [sum(src.shape[1] for src, _, _ in strips[:i]) for i in range(len(strips))]
    READY = [sum(src.shape[0] // P for src, _ in weights[:n + 1]) for n in range(len(weights))]
    PROJ_READY, W1_READY, W2_READY, W3_READY = READY
    strip_in = [mem.sem(f"strip_in{i}") for i in range(8)]
    w_hi, w_split = mem.sem("mlp_w_hi"), mem.sem("mlp_w_split")

    def strip(i):
        at_col, width = strip_at[i] % RING_WORDS, strips[i][0].shape[1]
        return ring[:, at_col:at_col + width]

    const_in, ga_in, gb_in = mem.sem("const_in"), mem.sem("ga_in"), mem.sem("gb_in")
    at_in = mem.sem("at_in")
    res_in = [mem.sem(f"res_in{h}") for h in range(HALVES)]
    out_done = [mem.sem(f"out_done{h}") for h in range(HALVES)]
    (f_done, f_act, f_hi, f_split, t_done, t_act, t_taken, gate_step, x2_ready, stats_done, aggr_done, var_ready,
     rstd_ready, x_norm, mod_ready, out_step, out_ready, consts) = (mem.sem(n) for n in (
         "f_done", "f_act", "f_hi", "f_split", "t_done", "t_act", "t_taken", "gate_step", "x2_ready",
         "mlp_stats_done", "mlp_aggr_done", "mlp_var_ready", "mlp_rstd_ready", "mlp_x_norm", "mlp_mod_ready",
         "out_step", "out_ready", "mlp_consts"))
    F_CREDITS, FULL_CREDITS, T_CREDITS = 4, 2, 4

    def rows_no(k, c):
        return FB * k + c

    def layer_no(k, layer, f):
        return FB * k + NC_ + NF * (layer - 1) + f

    def turned_no(k, c):
        return TB * k + c if k_is_first(k) else TB * k - CT + c

    def k_is_first(k):
        return isinstance(k, int) and k == 0

    def proj_no(k, t):
        return turned_no(k, NC_) + t

    def last_no(k, t, more):
        return TB * k + NC_ + CT + (NC_ + CT if more else 0) + t

    def over_chunks(engine, body):
        for half in range(HALVES):
            body(half, 0, half, True)
        with engine.Fori(1, B - 1) as b:
            for half in range(HALVES):
                body(HALVES * b + half, b, half, True)
        for half in range(HALVES):
            body(HALVES * (B - 1) + half, B - 1, half, half < HALVES - 1)

    def following(b, half):
        return (b, half + 1) if half < HALVES - 1 else (b + 1, 0)

    def fbank_of(k_even_no):
        return fbank[k_even_no % 4]

    def tiles(dram, b, half):
        return dram[b, half * CH:(half + 1) * CH, :].rearrange("(t p) n -> p t n", p=P)

    with nc.Block() as block:
        @block.sync
        def _(sp):
            def load_gate(tile, b, which, sem):
                sp.dma_start(tile[:], gate_dram[b:b + 1, which * C:(which + 1) * C].to_broadcast([P, C])
                             if isinstance(b, int) else
                             gate_dram[bass.ds(b, 1), which * C:(which + 1) * C].to_broadcast([P, C])).then_inc(sem, 16)

            def load_attn(b, half):
                sp.dma_start(at[:], tiles(attn_dram, b, half)).then_inc(at_in, 16)

            def load_x(b, half):
                sp.dma_start(xt[:, half], tiles(x, b, half)).then_inc(res_in[half], 16)

            held = (out_done[0], 16)
            load_attn(0, 0)
            for i, (src, _, c) in enumerate(strips):
                over = strip_at[i] + src.shape[1] - RING_WORDS
                if over > 0:
                    sp.wait_ge(w_split, sum(a < over for a in strip_at))
                sp.dma_start(strip(i), src[c * P:(c + 1) * P, :]).then_inc(strip_in[i % 8], 16)
                if i == PROJ_READY - 1:
                    load_x(0, 0)
                    load_gate(ga, 0, 0, ga_in)
                    sp.dma_start(b1_cols[:], b1_c).then_inc(const_in, 16)
                if i == W1_READY + 3:
                    sp.wait_ge(f_done, rows_no(0, NC_))
                    load_attn(0, 1)
                if i == W1_READY + 1:
                    load_gate(gb, 0, 1, gb_in)
                    sp.dma_start(b2_cols[:], b2_c).then_inc(const_in, 16)
                    sp.dma_start(b3_rows[:], b3.to_broadcast([P, C])).then_inc(const_in, 16)

            def chunk(k, b, half, more):
                nb, nh = following(b, half)
                if more:
                    if not (k_is_first(k)):
                        wait_apart(sp, f_done, rows_no(k, NC_), held)
                        load_attn(nb, nh)
                    wait_apart(sp, out_done[nh], 16 * (b + half + 1), held)
                    load_x(nb, nh)
                    if nh == 0:
                        wait_apart(sp, t_taken, T_CREDITS + proj_no(k, CT), held)
                        load_gate(ga, nb, 0, ga_in)
                if more and nh == 0:
                    sp.wait_ge(out_ready, CT * (k + 1))
                    load_gate(gb, nb, 1, gb_in)

            over_chunks(sp, chunk)

        @block.gpsimd
        def _(pool):
            nc.gpsimd.memset(minus_half[:], -0.5).then_inc(consts, 1)
            pool.wait_ge(consts, 1)

            def inverse_deviation(k):
                pool.wait_ge(var_ready, k + 1)
                nc.gpsimd.tensor_tensor(rstd[:], var_eps[:], minus_half[:], ALU.pow).then_inc(rstd_ready, 1)

            inverse_deviation(0)

            def chunk(k, b, half, more):
                if more:
                    inverse_deviation(k + 1)

            over_chunks(pool, chunk)

        @block.scalar
        def _(act):
            act.sem_inc(f_act, F_CREDITS)
            for half in range(HALVES):
                act.sem_inc(out_done[half], 16)

            def turned_hi(k, c, at_no):
                act.wait_ge(t_done, turned_no(k, c) + 1)
                nc.scalar.copy(a[:, 0, c, :], tbank[at_no % 4][:, 0:CH]).then_inc(t_act, 1)

            def modulate(k, b, c):
                act.wait_ge(f_done, rows_no(k, c) + 1)
                act.wait_ge(f_split, rows_no(k, c) + 1)
                if c == 0:
                    act.wait_ge(mod_ready, b + 1)
                nc.scalar.activation(full[:, c % 2, :], fbank[c % 4][:, 0:CH], ACT.Identity,
                                     scale=mod_now[:, NC_ + c:NC_ + c + 1], bias=mod_now[:, c:c + 1])\
                    .then_inc(f_act, 1)

            def hidden(k, layer, f):
                act.wait_ge(f_done, layer_no(k, layer, f) + 1)
                act.wait_ge(f_split, layer_no(k, layer, f) + 1)
                bias = (b1_cols, b2_cols)[layer - 1]
                nc.scalar.activation(full[:, f % 2, :], fbank[f % 4][:, 0:CH], ACT.Relu, bias=bias[:, f:f + 1])\
                    .then_inc(f_act, 1)

            def strips_hi(first, end):
                for i in range(first, end):
                    act.wait_ge(strip_in[i % 8], 16 * (i // 8 + 1))
                    nc.scalar.copy(strips[i][1][:, 0, strips[i][2], :], strip(i)).then_inc(w_hi, 1)

            strips_hi(0, PROJ_READY)
            for c in range(NC_):
                turned_hi(0, c, c)
            strips_hi(PROJ_READY, W1_READY)
            for c in range(NC_):
                modulate(0, 0, c)
            act.wait_ge(const_in, 48)

            def chunk(k, b, half, more):
                nb, nh = following(b, half)
                for f in range(NF):
                    hidden(k, 1, f)
                    if k_is_first(k):
                        strips_hi(W1_READY + f, W1_READY + f + 1)
                if k_is_first(k):
                    strips_hi(W2_READY, W3_READY)
                if more:
                    for c in range(NC_):
                        turned_hi(k + 1, c, turned_no(1, c))
                for f in range(NF):
                    hidden(k, 2, f)
                if more:
                    for c in range(NC_):
                        modulate(k + 1, nb, c)
                act.wait_ge(out_ready, CT * (k + 1))
                act.dma_start(tiles(out, b, half), xt[:, half]).then_inc(out_done[half], 16)

            over_chunks(act, chunk)
            for half in range(HALVES):
                act.wait_ge(out_done[half], 16 * (B + 1))

        @block.vector
        def _(dve):
            dve.sem_inc(f_split, FULL_CREDITS)
            dve.sem_inc(t_taken, T_CREDITS)

            def turned_lo(k, c, at_no):
                dve.wait_ge(t_act, NC_ * k + c + 1)
                nc.vector.tensor_tensor(a[:, 1, c, :], tbank[at_no % 4][:, 0:CH], f32(a[:, 0, c, :]), ALU.subtract)\
                    .then_inc(t_taken, 1)

            def split(dst, c, number, ring):
                dve.wait_ge(f_act, F_CREDITS + number + 1)
                nc.vector.tensor_copy(dst[:, 0, c, :], full[:, ring, :]).then_inc(f_hi, 1)
                dve.wait_ge(f_hi, number + 1)
                nc.vector.tensor_tensor(dst[:, 1, c, :], full[:, ring, :], f32(dst[:, 0, c, :]), ALU.subtract)\
                    .then_inc(f_split, 1)

            def add_attention(k, b, half, t, at_no):
                dve.wait_ge(t_done, proj_no(k, t) + 1)
                if half == 0 and t == 0:
                    dve.wait_ge(ga_in, 16 * (b + 1))
                nc.vector.tensor_tensor(gated[:], tbank[at_no % 4][:], ga[:], ALU.mult).then_inc(t_taken, 1)
                dve.wait_ge(t_taken, T_CREDITS + proj_no(k, t) + 1)
                dve.wait_ge(res_in[half], 16 * (b + 1))
                nc.vector.tensor_tensor(xt[:, half, t, :], xt[:, half, t, :], gated[:], ALU.add).then_inc(x2_ready, 1)
                dve.wait_ge(x2_ready, CT * k + t + 1)
                nc.vector.bn_stats(stats[:, t, :], xt[:, half, t, :]).then_inc(stats_done, 1)
                dve.drain()
                nc.vector.bn_aggr(mean_var[:, t, :], stats[:, t, :]).then_inc(aggr_done, 1)

            def variance(k):
                dve.wait_ge(aggr_done, CT * (k + 1))
                nc.vector.tensor_scalar_add(var_eps[:], mean_var[:, :, 1], EPS).then_inc(var_ready, 1)

            def normalise(k, b, half):
                dve.wait_ge(rstd_ready, k + 1)
                for t in range(CT):
                    nc.vector.tensor_scalar(at[:, t, :], xt[:, half, t, :], mean_var[:, t, 0:1], rstd[:, t:t + 1],
                                            ALU.subtract, ALU.mult).then_inc(x_norm, 1)
                if half == 0:
                    nc.vector.tensor_copy(mod_now[:], mod_cols[:, 1, :, b]).then_inc(mod_ready, 1)

            def finish(k, b, half, t, more):
                dve.wait_ge(t_done, last_no(k, t, more) + 1)
                if half == 0 and t == 0:
                    dve.wait_ge(gb_in, 16 * (b + 1))
                if t:
                    dve.wait_ge(out_ready, CT * k + t)
                nc.vector.tensor_tensor(gated[:], tbank[last_no(0, t, more) % 4][:], b3_rows[:], ALU.add).then_inc(t_taken, 1)
                dve.wait_ge(t_taken, T_CREDITS + last_no(k, t, more) + 1)
                nc.vector.tensor_tensor(gated[:], gated[:], gb[:], ALU.mult).then_inc(out_step, 1)
                dve.wait_ge(out_step, CT * k + t + 1)
                nc.vector.tensor_tensor(xt[:, half, t, :], xt[:, half, t, :], gated[:], ALU.add).then_inc(out_ready, 1)

            def strips_lo(first, end):
                for i in range(first, end):
                    _, dst, c = strips[i]
                    dve.wait_ge(w_hi, i + 1)
                    nc.vector.tensor_tensor(dst[:, 1, c, :], strip(i), f32(dst[:, 0, c, :]), ALU.subtract)\
                        .then_inc(w_split, 1)

            strips_lo(0, PROJ_READY)
            for c in range(NC_):
                turned_lo(0, c, c)
            for t in range(CT):
                add_attention(0, 0, 0, t, NC_ + t)
            variance(0)
            normalise(0, 0, 0)
            strips_lo(PROJ_READY, W1_READY)
            for c in range(NC_):
                split(a, c, rows_no(0, c), c % 2)
            dve.wait_ge(const_in, 48)

            def chunk(k, b, half, more):
                nb, nh = following(b, half)
                for f in range(NF):
                    split(y1, f, layer_no(k, 1, f), f % 2)
                    if k_is_first(k):
                        strips_lo(W1_READY + f, W1_READY + f + 1)
                if k_is_first(k):
                    strips_lo(W2_READY, W3_READY)
                    dve.wait_ge(w_split, W3_READY)
                if more:
                    for c in range(NC_):
                        turned_lo(k + 1, c, turned_no(1, c))
                for f in range(NF):
                    split(y2, f, layer_no(k, 2, f), f % 2)
                    if more and f == PROJ_AFTER - 1:
                        for t in range(CT):
                            add_attention(k + 1, nb, nh, t, proj_no(1, t))
                        variance(k + 1)
                    if more and f == NORM_AFTER - 1:
                        normalise(k + 1, nb, nh)
                if more:
                    for c in range(NC_):
                        split(a, c, rows_no(k + 1, c), c % 2)
                for t in range(CT):
                    finish(k, b, half, t, more)

            over_chunks(dve, chunk)

        @block.tensor
        def _(pe):
            def turn_attention(k, c, at_no):
                if c == 0:
                    pe.wait_ge(at_in, 16 * (k + 1))
                pe.wait_ge(t_taken, turned_no(k, c) + 1)
                for t in range(CT):
                    mm = nc.tensor.transpose(tbank[at_no % 4][:, t * P:(t + 1) * P], at[:, t, c * P:(c + 1) * P],
                                             ident[:])
                mm.then_inc(t_done, 1)

            def turn_rows(k, c):
                if c == 0:
                    pe.wait_ge(x_norm, CT * (k + 1))
                pe.wait_ge(f_act, rows_no(k, c) + 1)
                for t in range(CT):
                    mm = nc.tensor.transpose(fbank[c % 4][:, t * P:(t + 1) * P], at[:, t, c * P:(c + 1) * P], ident[:])
                mm.then_inc(f_done, 1)

            def token_rows(weights, data, chunks, t, bank, number, ready):
                pe.wait_ge(t_taken, number + 1)
                for c in range(chunks):
                    if t == 0:
                        ready(c)
                    for i, (wl, dl) in enumerate(TERMS):
                        mm = nc.tensor.matmul(bank[:], data[:, dl, c, t * P:(t + 1) * P], weights[:, wl, c, :],
                                              start=(c == 0 and i == 0), stop=(c == chunks - 1 and i == 2))
                mm.then_inc(t_done, 1)

            def project(k, t, at_no):
                token_rows(wproj, a, NC_, t, tbank[at_no % 4], proj_no(k, t),
                           lambda c: pe.wait_ge(t_taken, T_CREDITS + turned_no(k, c) + 1))

            def last_layer(k, t, more):
                token_rows(w3, y2, NF, t, tbank[last_no(0, t, more) % 4], last_no(k, t, more),
                           lambda c: pe.wait_ge(f_split, FULL_CREDITS + layer_no(k, 2, c) + 1))

            def hidden(k, layer, f):
                weights, data, chunks = ((w1, a, NC_), (w2, y1, NF))[layer - 1]
                pe.wait_ge(f_act, layer_no(k, layer, f) + 1)
                for c in range(chunks):
                    if f == 0:
                        pe.wait_ge(f_split, FULL_CREDITS + 1 + (rows_no(k, c) if layer == 1 else layer_no(k, 1, c)))
                    for i, (wl, dl) in enumerate(TERMS):
                        mm = nc.tensor.matmul(fbank[f % 4][:, 0:CH], weights[:, wl, c, f * P:(f + 1) * P],
                                              data[:, dl, c, :], start=(c == 0 and i == 0),
                                              stop=(c == chunks - 1 and i == 2))
                mm.then_inc(f_done, 1)

            for c in range(NC_):
                turn_attention(0, c, c)
            pe.wait_ge(w_split, PROJ_READY)
            for t in range(CT):
                project(0, t, NC_ + t)
            for c in range(NC_):
                turn_rows(0, c)
            pe.wait_ge(w_split, W1_READY)

            def chunk(k, b, half, more):
                for f in range(NF):
                    hidden(k, 1, f)
                if more:
                    for c in range(NC_):
                        turn_attention(k + 1, c, turned_no(1, c))
                if k_is_first(k):
                    pe.wait_ge(w_split, W2_READY)
                for f in range(NF):
                    hidden(k, 2, f)
                    if more and f == PROJ_AFTER - 1:
                        for t in range(CT):
                            project(k + 1, t, proj_no(1, t))
                if more:
                    for c in range(NC_):
                        turn_rows(k + 1, c)
                if k_is_first(k):
                    pe.wait_ge(w_split, W3_READY)
                for t in range(CT):
                    last_layer(k, t, more)

            over_chunks(pe, chunk)


def kernel(L0_attn_x, L0_attn_W_attn, L0_attn_W_proj, L0_ffn_W1, L0_ffn_b1, L0_ffn_W2, L0_ffn_b2, L0_ffn_W3,
           L0_ffn_b3, L0_c, L0_wmod):
    import numpy as np
    import concourse.bacc as bacc
    from concourse.bass_utils import run_bass_kernel_spmd

    arrays = {
        "x": L0_attn_x, "wqkv_t": np.asarray(L0_attn_W_attn).T, "wproj_t": np.asarray(L0_attn_W_proj).T,
        "w1_t": np.asarray(L0_ffn_W1).T, "b1_c": np.asarray(L0_ffn_b1).reshape(NF, P).T,
        "w2_t": np.asarray(L0_ffn_W2).T, "b2_c": np.asarray(L0_ffn_b2).reshape(NF, P).T,
        "w3_t": np.asarray(L0_ffn_W3).T, "b3": np.asarray(L0_ffn_b3).reshape(1, C),
        "c_t": np.asarray(L0_c).T, "wmod": L0_wmod,
    }
    arrays = {k: np.ascontiguousarray(a) for k, a in arrays.items()}
    nc = bacc.Bacc("TRN2", target_bir_lowering=False, num_devices=1)
    ins = {k: nc.dram_tensor(k, a.shape, mybir.dt.from_np(a.dtype), kind="ExternalInput").ap()
           for k, a in arrays.items()}
    attn_dram = nc.dram_tensor("attn_dram", (B, T, C), F32, kind="Internal").ap()
    gate_dram = nc.dram_tensor("gate_dram", (B, 2 * C), F32, kind="Internal").ap()
    out = nc.dram_tensor("out", (B, T, C), F32, kind="ExternalOutput").ap()
    build(nc, attn_dram=attn_dram, gate_dram=gate_dram, out=out, **ins)
    result = run_bass_kernel_spmd(nc, [arrays], core_ids=[0])
    return result.results[0]["out"]
```
